# Optimizing a Trainium2 kernel written in Bass

```python
import numpy as np
import jax
import jax.numpy as jnp

def _softmax(x, axis=-1):
    return jax.nn.softmax(x, axis=axis)

def _gelu(x):
    return jax.nn.gelu(x, approximate=True)

def _silu(x):
    return jax.nn.silu(x)

def _sigmoid(x):
    return jax.nn.sigmoid(x)

def _layernorm(x, axis=-1, eps=1e-05):
    m = jnp.mean(x, axis=axis, keepdims=True)
    v = jnp.var(x, axis=axis, keepdims=True)
    return (x - m) / jnp.sqrt(v + eps)

def _scatter_add(tgt, idx, src, axis=0):
    return tgt.at[idx].add(src)

def _segment_sum(src, seg, n):
    return jax.ops.segment_sum(src, seg, n)
kernel_name = 'mk_cond_resid_d4_seqx_r8_bfd44a'

def setup_inputs(seed: int=0):
    np.random.seed(seed)
    _w = jnp.asarray

    def _rec_inputs():
        import jax
        import jax.numpy as jnp
        _rk = jax.random.key(seed)
        x = 4.136e-05 + 0.9999 * jax.random.normal(jax.random.fold_in(_rk, 1), (32, 128, 128), jnp.float32)
        _lenS = 128 - jax.random.randint(jax.random.fold_in(_rk, 7), (32,), 0, max(1, 128 // 4) + 1, jnp.int32)
        _lenS2 = 128 - jax.random.randint(jax.random.fold_in(_rk, 8), (32,), 0, max(1, 128 // 4) + 1, jnp.int32)
        cond_1024 = -0.00608245 + 1.00131 * jax.random.normal(jax.random.fold_in(_rk, 11), (32, 128), jnp.float32)
        return (x, cond_1024)
    x, cond_1024 = _rec_inputs()

    def _L0_cond_setup():
        import jax, jax.numpy as jnp
        import numpy as np
        B, T, D_IN, V_IN, E = (64, 128, 128, 128, 128)
        key = jax.random.key(seed)
        ks = jax.random.split(key, 16)
        s = 0.01
        return {'video': jax.random.normal(ks[0], (B, V_IN), jnp.float32), 'seq': jax.random.normal(ks[1], (B, T, D_IN), jnp.float32), 'W_z': jax.random.normal(ks[2], (D_IN, E), jnp.float32) * s, 'U_z': jax.random.normal(ks[3], (E, E), jnp.float32) * s, 'C_z': jax.random.normal(ks[4], (V_IN, E), jnp.float32) * s, 'b_z': jnp.zeros((E,), jnp.float32), 'W_r': jax.random.normal(ks[5], (D_IN, E), jnp.float32) * s, 'U_r': jax.random.normal(ks[6], (E, E), jnp.float32) * s, 'C_r': jax.random.normal(ks[7], (V_IN, E), jnp.float32) * s, 'b_r': jnp.zeros((E,), jnp.float32), 'W': jax.random.normal(ks[8], (D_IN, E), jnp.float32) * s, 'U': jax.random.normal(ks[9], (E, E), jnp.float32) * s, 'C': jax.random.normal(ks[10], (V_IN, E), jnp.float32) * s, 'b': jnp.zeros((E,), jnp.float32)}
    _L0_cond_all = _L0_cond_setup()
    _L0_cond_in = {k: v for k, v in _L0_cond_all.items() if k in ('W_z', 'U_z', 'C_z', 'b_z', 'W_r', 'U_r', 'C_r', 'b_r', 'W', 'U', 'C', 'b')}
    del _L0_cond_all

    def _L1_cond_setup():
        import jax, jax.numpy as jnp
        import numpy as np
        TOP_K = 2
        N_EXPERTS = 8
        N_SHARED = 1
        EPS = 1e-09
        key = jax.random.key(seed)
        ks = jax.random.split(key, 10)
        B, T, d = (2, 256, 128)
        h_s, h_r, E = (256, 64, N_EXPERTS)
        return {'x': jax.random.normal(ks[0], (B, T, d), jnp.float32), 't_emb': jax.random.normal(ks[1], (B, d), jnp.float32), 'router_w': jax.random.normal(ks[2], (E, d), jnp.float32) * 0.01, 'router_t_w': jax.random.normal(ks[3], (E, d), jnp.float32) * 0.01, 'router_bias': jnp.zeros((E,), jnp.float32), 'sw1': jax.random.normal(ks[4], (h_s, d), jnp.float32) * 0.02, 'sw3': jax.random.normal(ks[5], (h_s, d), jnp.float32) * 0.02, 'sw2': jax.random.normal(ks[6], (d, h_s), jnp.float32) * 0.02, 'rw1': jax.random.normal(ks[7], (E, h_r, d), jnp.float32) * 0.02, 'rw2': jax.random.normal(ks[8], (E, d, h_r), jnp.float32) * 0.02}
    _L1_cond_all = _L1_cond_setup()
    _L1_cond_in = {k: v for k, v in _L1_cond_all.items() if k in ('router_w', 'router_t_w', 'router_bias', 'sw1', 'sw3', 'sw2', 'rw1', 'rw2')}
    del _L1_cond_all

    def _L2_cond_setup():
        import jax, jax.numpy as jnp
        import numpy as np
        RANK = 8
        LN_EPS = 1e-05
        key = jax.random.key(seed)
        ks = jax.random.split(key, 8)
        B, T, D = (16, 128, 128)
        A = 128
        I = 128
        OUT = D * RANK * 4
        s = 0.02
        return {'x': jax.random.normal(ks[0], (B, T, D), jnp.float32), 'ada_emb': jax.random.normal(ks[1], (B, A), jnp.float32), 'base_up': jax.random.normal(ks[2], (D, D), jnp.float32) * s, 'base_down': jax.random.normal(ks[3], (D, D), jnp.float32) * s, 'ln_gamma': jnp.ones((A,), jnp.float32), 'ln_beta': jnp.zeros((A,), jnp.float32), 'W1': jax.random.normal(ks[4], (A, I), jnp.float32) / np.sqrt(A), 'bias1': jnp.zeros((I,), jnp.float32), 'W2': jax.random.normal(ks[5], (I, OUT), jnp.float32) / np.sqrt(I), 'bias2': jnp.zeros((OUT,), jnp.float32)}
    _L2_cond_all = _L2_cond_setup()
    _L2_cond_in = {k: v for k, v in _L2_cond_all.items() if k in ('base_up', 'base_down', 'ln_gamma', 'ln_beta', 'W1', 'bias1', 'W2', 'bias2')}
    del _L2_cond_all

    def _L3_cond_setup():
        import jax, jax.numpy as jnp
        import numpy as np
        N, T, D, H = (64, 64, 128, 128)
        key = jax.random.key(seed)
        k1, k2, k3, k4 = jax.random.split(key, 4)
        x = jax.random.normal(k1, (N, T, D), dtype=jnp.float32)
        h0 = jax.random.normal(k2, (N, H), dtype=jnp.float32)
        Wx = jax.random.normal(k3, (D, H), dtype=jnp.float32) / jnp.sqrt(jnp.float32(D))
        Wh = jax.random.normal(k4, (H, H), dtype=jnp.float32) / jnp.sqrt(jnp.float32(H))
        b = jnp.zeros((H,), dtype=jnp.float32)
        return {'x': x, 'h0': h0, 'Wx': Wx, 'Wh': Wh, 'b': b}
    _L3_cond_all = _L3_cond_setup()
    _L3_cond_in = {k: v for k, v in _L3_cond_all.items() if k in ('Wx', 'Wh', 'b')}
    del _L3_cond_all
    return {'x': x, 'cond_1024': cond_1024, 'L0_cond_W_z': _L0_cond_in['W_z'], 'L0_cond_U_z': _L0_cond_in['U_z'], 'L0_cond_C_z': _L0_cond_in['C_z'], 'L0_cond_b_z': _L0_cond_in['b_z'], 'L0_cond_W_r': _L0_cond_in['W_r'], 'L0_cond_U_r': _L0_cond_in['U_r'], 'L0_cond_C_r': _L0_cond_in['C_r'], 'L0_cond_b_r': _L0_cond_in['b_r'], 'L0_cond_W': _L0_cond_in['W'], 'L0_cond_U': _L0_cond_in['U'], 'L0_cond_C': _L0_cond_in['C'], 'L0_cond_b': _L0_cond_in['b'], 'L1_cond_router_w': _L1_cond_in['router_w'], 'L1_cond_router_t_w': _L1_cond_in['router_t_w'], 'L1_cond_router_bias': _L1_cond_in['router_bias'], 'L1_cond_sw1': _L1_cond_in['sw1'], 'L1_cond_sw3': _L1_cond_in['sw3'], 'L1_cond_sw2': _L1_cond_in['sw2'], 'L1_cond_rw1': _L1_cond_in['rw1'], 'L1_cond_rw2': _L1_cond_in['rw2'], 'L2_cond_base_up': _L2_cond_in['base_up'], 'L2_cond_base_down': _L2_cond_in['base_down'], 'L2_cond_ln_gamma': _L2_cond_in['ln_gamma'], 'L2_cond_ln_beta': _L2_cond_in['ln_beta'], 'L2_cond_W1': _L2_cond_in['W1'], 'L2_cond_bias1': _L2_cond_in['bias1'], 'L2_cond_W2': _L2_cond_in['W2'], 'L2_cond_bias2': _L2_cond_in['bias2'], 'L3_cond_Wx': _L3_cond_in['Wx'], 'L3_cond_Wh': _L3_cond_in['Wh'], 'L3_cond_b': _L3_cond_in['b']}

def reference(x, cond_1024, L0_cond_W_z, L0_cond_U_z, L0_cond_C_z, L0_cond_b_z, L0_cond_W_r, L0_cond_U_r, L0_cond_C_r, L0_cond_b_r, L0_cond_W, L0_cond_U, L0_cond_C, L0_cond_b, L1_cond_router_w, L1_cond_router_t_w, L1_cond_router_bias, L1_cond_sw1, L1_cond_sw3, L1_cond_sw2, L1_cond_rw1, L1_cond_rw2, L2_cond_base_up, L2_cond_base_down, L2_cond_ln_gamma, L2_cond_ln_beta, L2_cond_W1, L2_cond_bias1, L2_cond_W2, L2_cond_bias2, L3_cond_Wx, L3_cond_Wh, L3_cond_b):
    import jax
    import jax.numpy as jnp

    def _L0_cond_ref(video, seq, W_z, U_z, C_z, b_z, W_r, U_r, C_r, b_r, W, U, C, b):
        import jax, jax.numpy as jnp
        import numpy as np
        B, T, D_IN, V_IN, E = (64, 128, 128, 128, 128)
        vz = video @ C_z + b_z
        vr = video @ C_r + b_r
        vh = video @ C + b
        xz = jnp.einsum('btd,de->bte', seq, W_z)
        xr = jnp.einsum('btd,de->bte', seq, W_r)
        xh = jnp.einsum('btd,de->bte', seq, W)

        def step(h, xs):
            xzt, xrt, xht = xs
            z = jax.nn.sigmoid(xzt + h @ U_z + vz)
            r = jax.nn.sigmoid(xrt + h @ U_r + vr)
            hh = jnp.tanh(xht + r * h @ U + vh)
            h_new = (1.0 - z) * h + z * hh
            return (h_new, h_new)
        h0 = jnp.zeros((seq.shape[0], U.shape[0]), seq.dtype)
        xs = (jnp.swapaxes(xz, 0, 1), jnp.swapaxes(xr, 0, 1), jnp.swapaxes(xh, 0, 1))
        _, out_t = jax.lax.scan(step, h0, xs)
        return jnp.swapaxes(out_t, 0, 1)

    def _L1_cond_ref(x, t_emb, router_w, router_t_w, router_bias, sw1, sw3, sw2, rw1, rw2):
        import jax, jax.numpy as jnp
        import numpy as np
        TOP_K = 2
        N_EXPERTS = 8
        N_SHARED = 1
        EPS = 1e-09
        B, T, C = x.shape
        N = B * T
        x_flat = x.reshape(N, C)
        shared_out = jnp.einsum('nh,dh->nd', jax.nn.silu(x_flat @ sw1.T) * (x_flat @ sw3.T), sw2)
        t_bias = t_emb @ router_t_w.T
        t_bias_flat = jnp.broadcast_to(t_bias[:, None, :], (B, T, N_EXPERTS)).reshape(N, N_EXPERTS)
        s = jax.nn.sigmoid((x_flat @ router_w.T + t_bias_flat).astype(jnp.float32))
        sel_scores = s + router_bias
        _, topk_idx = jax.lax.top_k(sel_scores, TOP_K)
        s_sel = jnp.take_along_axis(s, topk_idx, axis=1)
        denom = jnp.sum(s_sel, axis=1, keepdims=True)
        gates = jnp.where(denom > EPS, s_sel / (denom + EPS), 1.0 / TOP_K).astype(x.dtype)
        combine = jnp.sum(gates[:, :, None] * jax.nn.one_hot(topk_idx, N_EXPERTS, dtype=x.dtype), axis=1)
        H = jax.nn.gelu(jnp.einsum('nd,ehd->enh', x_flat, rw1), approximate=False)
        O = jnp.einsum('enh,edh->end', H, rw2)
        routed_out = jnp.einsum('end,ne->nd', O, combine)
        out = (shared_out + routed_out) / (N_SHARED + TOP_K)
        return out.reshape(B, T, C)

    def _L2_cond_ref(x, ada_emb, base_up, base_down, ln_gamma, ln_beta, W1, bias1, W2, bias2):
        import jax, jax.numpy as jnp
        import numpy as np
        RANK = 8
        LN_EPS = 1e-05
        B, T, D = x.shape
        R = RANK
        mu = jnp.mean(ada_emb, axis=-1, keepdims=True)
        var = jnp.mean(jnp.square(ada_emb - mu), axis=-1, keepdims=True)
        c = (ada_emb - mu) / jnp.sqrt(var + LN_EPS) * ln_gamma + ln_beta
        h = jax.nn.gelu(c @ W1 + bias1, approximate=False)
        w = h @ W2 + bias2
        a1, b1, a2, b2 = [t.reshape(B, D, R) for t in jnp.split(w, 4, axis=-1)]
        u = jnp.einsum('btd,bdr->btr', x, a2)
        mid = jnp.einsum('btd,dl->btl', x, base_down) + jnp.einsum('btr,blr->btl', u, b2)
        mid = jax.nn.gelu(mid, approximate=False)
        v = jnp.einsum('blr,btl->btr', b1, mid)
        out = jnp.einsum('btl,kl->btk', mid, base_up) + jnp.einsum('bkr,btr->btk', a1, v)
        return x + out

    def _L3_cond_ref(x, h0, Wx, Wh, b):
        import jax, jax.numpy as jnp
        import numpy as np
        N, T, D, H = (64, 64, 128, 128)
        xw = jnp.einsum('ntd,dh->nth', x, Wx) + b

        def step(prev_h, xw_t):
            next_h = jnp.tanh(xw_t + prev_h @ Wh)
            return (next_h, next_h)
        _, hs = jax.lax.scan(step, h0, jnp.swapaxes(xw, 0, 1))
        return jnp.swapaxes(hs, 0, 1)
    x = x + _L0_cond_ref(cond_1024, x, L0_cond_W_z, L0_cond_U_z, L0_cond_C_z, L0_cond_b_z, L0_cond_W_r, L0_cond_U_r, L0_cond_C_r, L0_cond_b_r, L0_cond_W, L0_cond_U, L0_cond_C, L0_cond_b)
    x = x + _L1_cond_ref(x, cond_1024, L1_cond_router_w, L1_cond_router_t_w, L1_cond_router_bias, L1_cond_sw1, L1_cond_sw3, L1_cond_sw2, L1_cond_rw1, L1_cond_rw2)
    x = x + _L2_cond_ref(x, cond_1024, L2_cond_base_up, L2_cond_base_down, L2_cond_ln_gamma, L2_cond_ln_beta, L2_cond_W1, L2_cond_bias1, L2_cond_W2, L2_cond_bias2)
    x = x + _L3_cond_ref(x, cond_1024, L3_cond_Wx, L3_cond_Wh, L3_cond_b)
    return x

_drawn_inputs = setup_inputs


def setup_inputs(seed=0):
    import zlib

    import numpy as np

    out = dict(_drawn_inputs(seed))
    spreads = {'L0_cond_b_z': (0.0, 2.0),
     'L0_cond_b_r': (0.0, 2.0),
     'L0_cond_b': (0.0, 0.1),
     'L1_cond_router_bias': (0.0, 0.8),
     'L2_cond_ln_gamma': (1.0, 0.2),
     'L2_cond_ln_beta': (0.0, 0.1),
     'L2_cond_bias1': (0.0, 0.1),
     'L2_cond_bias2': (0.0, 0.1),
     'L3_cond_b': (0.0, 2.0)}
    factors = {'L0_cond_W_z': 8.0,
     'L0_cond_U_z': 64.0,
     'L0_cond_C_z': 8.0,
     'L0_cond_W_r': 22.005,
     'L0_cond_U_r': 64.0,
     'L0_cond_C_r': 25.228,
     'L0_cond_U': 6.7,
     'L1_cond_router_w': 8.0,
     'L1_cond_router_t_w': 8.0,
     'L1_cond_sw1': 8.0,
     'L1_cond_sw3': 8.0,
     'L1_cond_sw2': 8.0,
     'L1_cond_rw1': 8.0,
     'L1_cond_rw2': 8.0,
     'L2_cond_base_up': 3.975,
     'L2_cond_base_down': 3.744,
     'L3_cond_Wx': 200.0,
     'L3_cond_Wh': 200.0}
    for name, (base, spread) in spreads.items():
        noise = np.random.default_rng([zlib.crc32(name.encode()), seed]).standard_normal(out[name].shape)
        drawn = base * np.exp(spread * noise) if base else spread * noise
        out[name] = jnp.asarray(drawn.astype(out[name].dtype))
    for name, factor in factors.items():
        out[name] = (out[name] * factor).astype(out[name].dtype)
    return out
```

```python
import concourse.bass as bass
from concourse import mybir
from contextlib import ExitStack

B, T, D = 32, 128, 128
NE, HR, HS = 8, 64, 256
R = 8
ST = 8
NC = T // ST
CB = ST * B
GB = 16
ROUTER_EPS = 1e-9
LN_EPS = 1e-5
EULER = 2.718281828459045

V_R, V_Z, V_H, V_T, V_B, V_END = 0, 128, 256, 384, 392, 520
G_COND = 0
G_C = 96
G_W = G_C + 392
G_U = G_W + 384
G_END = G_U + 384
M_SW1, M_SW3, M_RW1, M_SW2, M_RW2, M_RT, M_RB = 0, 256, 512, 1024, 1280, 1792, 1800
M_END = M_RB + 16
A_DOWN, A_UP, A_W1, A_GAMMA, A_BETA, A_BIAS1, A_BIAS2, A_WX, A_WH = 0, 128, 256, 384, 385, 386, 387, 419, 547
A_END = A_WH + 128
K_ID, K_HOT, K_MASK, K_LT = 0, 128, 128 + CB, 128 + CB + GB
K_END = K_LT + NE * NE
A1, B1, A2, B2 = range(4)


def recurrent_stack_kernel(nc, x_t, gru_pack, add_rows, cond_nat, moe_pack, ada_pack, w2_pack, const_pack, out_t):
    f32, bf16 = mybir.dt.float32, mybir.dt.bfloat16
    ALU, ACT, AX = mybir.AluOpType, mybir.ActivationFunctionType, mybir.AxisListType

    ctx = ExitStack()
    with ctx:
        def sb(name, shape, dt=f32):
            return ctx.enter_context(nc.sbuf_tensor(name, shape, dt))

        def bank(name):
            return ctx.enter_context(nc.psum_tensor(name, [128, 512], f32))

        def sem(name):
            return ctx.enter_context(nc.semaphore(name))

        gru = sb("gru", [128, G_END])
        rows = sb("rows", [1, V_END])
        ones = sb("ones", [1, 96])
        cond = sb("cond", [B, D])
        moe = sb("moe", [128, M_END])
        ada = sb("ada", [128, A_END])
        w2 = sb("w2", [128, 4, R, D])
        const = sb("const", [128, K_END])
        ident = const[:, K_ID:K_ID + 128]
        hot = sb("hot", [96, CB], bf16)
        vparts = sb("vparts", [96, V_END], bf16)
        vres = sb("vres", [96, V_END])
        vtop = sb("vtop", [96, V_END], bf16)
        vtop2 = sb("vtop2", [96, V_END], bf16)
        adapt = sb("adapt", [128, 4, B, R])
        adapt_t = sb("adapt_t", [128, 2, 2, 128])
        u_scaled = sb("u_scaled", [128, 3 * D])
        table_load = sb("table_load", [1, 1])
        euler, ones_wide = sb("euler", [128, 2 * NE]), sb("ones_wide", [128, 2 * NE])
        neglog, expneg = sb("neglog", [128, 2 * NE]), sb("expneg", [128, 2, 2 * NE])
        lnbuf = sb("lnbuf", [B, 4, D])
        lnstat = sb("lnstat", [B, 8])
        adah = sb("adah", [128, 4, B])
        xin = [sb(f"xin{p}", [128, CB]) for p in range(2)]
        hist = [sb(f"hist{p}", [128, CB]) for p in range(2)]
        x0 = [sb(f"x0_{p}", [128, CB]) for p in range(2)]
        x1 = sb("x1", [128, CB])
        x2 = [sb(f"x2_{p}", [128, CB]) for p in range(2)]
        rnn = [sb(f"rnn{p}", [128, CB]) for p in range(2)]
        yout = [sb(f"yout{p}", [128, CB]) for p in range(2)]
        rgate, zgate, cand = sb("rgate", [128, B]), sb("zgate", [128, B]), sb("cand", [128, B])
        rh, keep, take = sb("rh", [128, B]), sb("keep", [128, B]), sb("take", [128, B])
        shared = sb("shared", [128, 2, CB])
        hid = sb("hid", [128, 4, CB])
        sel = sb("sel", [128, 3, 2, NE])
        pair = sb("pair", [128, 3, 2, NE, NE])
        gst = sb("gst", [128, 8, 2])
        gmask = sb("gmask", [128, 4, 2, NE])
        gates = sb("gates", [128, 2, NE])
        gates_wide = [sb(f"gates_wide{k}", [128, 2, NE // 2, HR]) for k in range(2)]
        proj = sb("proj", [128, 2, ST, GB])
        mid = sb("mid", [128, CB])

        ps_rh = [bank(f"ps_rh{p}") for p in range(2)]
        ps_z = [bank(f"ps_z{p}") for p in range(2)]
        ps_n = bank("ps_n")
        ps_a, ps_b, ps_c = bank("ps_a"), bank("ps_b"), bank("ps_c")

        s_cond_w, s_gru, s_rows, s_cond, s_moe, s_ada, s_const, s_h30 = (
            sem(n) for n in ("cond_weights_loaded", "gru_loaded", "rows_loaded", "cond_loaded", "moe_loaded",
                             "ada_loaded", "const_loaded", "rnn_start_loaded"))
        s_w2 = [sem(f"w2_loaded{m}") for m in range(4)]
        x_loaded = [sem(f"x_loaded{p}") for p in range(2)]
        y_stored = [sem(f"y_stored{p}") for p in range(2)]
        s_ones, s_hot, h_zero, s_half = (sem(n) for n in ("ones_ready", "hot_ready", "h_start_ready", "half_ready"))
        v_mm, setup_chain, v_ready = sem("v_matmul_done"), sem("setup_chain"), sem("v_parts_ready")
        ln_dve, ln_pow, ln_tp = sem("ln_dve"), sem("ln_rsqrt_done"), sem("ln_transposed")
        c_ready, h2_mm, h2_ready = (sem(n) for n in ("ln_out_ready", "ada_hidden_mm", "ada_hidden_ready"))
        w_mm, w_out, t_mm, t_out, u_ready = (sem(n) for n in (
            "adapter_mm", "adapter_ready", "adapter_transposed", "adapter_t_ready", "u_scaled_ready"))
        LN_VAR, LN_OUT = 6, 7
        r_mm, z_mm, c_mm = sem("reset_mm"), sem("update_mm"), sem("cand_mm")
        r_ready, z_ready, cand_ready = sem("reset_ready"), sem("update_ready"), sem("cand_ready")
        rh_ready, keep_ready, take_ready, h_ready = (sem(n) for n in (
            "reset_h_ready", "keep_ready", "take_ready", "h_ready"))
        n_mm, n_ready = sem("rnn_mm"), sem("rnn_ready")
        x0_ready, router_mm, neg_ready, exp_ready, sum_ready, gate_chain, gates_ready = (sem(n) for n in (
            "x0_ready", "router_mm", "neg_logits_ready", "exp_ready", "exp_plus_one_ready", "gates_chain",
            "gates_ready"))
        sw1_mm, sw3_mm, sig_ready, sa_ready, shared_ready = (sem(n) for n in (
            "sw1_mm", "sw3_mm", "sigmoid_ready", "silu_ready", "shared_hidden_ready"))
        wide_ready = sem("gates_wide_half")
        rw1_mm, gelu_ready, gate_tp, hid_ready = (sem(n) for n in (
            "rw1_mm_half", "gelu_half", "gates_transposed_half", "hidden_half"))
        moe_mm, x1_ready = sem("moe_out_mm"), sem("x1_ready")
        down_mm, um_ready, pre_mm, mid_ready = (sem(n) for n in (
            "down_and_u_mm", "u_masked", "mid_pre_mm", "mid_ready"))
        up_mm, vm_ready, ada_mm, x2_ready, y_ready = (sem(n) for n in (
            "up_and_v_mm", "v_masked", "adapter_out_mm", "x2_ready", "y_ready"))

        mask = const[:, K_MASK:K_MASK + GB]
        lt = const[:, K_LT:K_LT + NE * NE].rearrange("p (e j) -> p e j", e=NE)

        def cols(s, n=1):
            return slice(s * B, (s + n) * B)

        def has(c, lag):
            return not isinstance(c, int) or 0 <= c - lag < NC

        FIRST_LOOP, LAST_LOOP = 5, 14
        GATE_STEPS = 18
        RNN_EARLY = 3

        def RNN_STEP(c, s):
            return c * ST + (s + RNN_EARLY - 3 * ST)


        def run_iterations(iteration, eng):
            for c in range(FIRST_LOOP):
                iteration(c // 2, c % 2)
            with eng.Fori(0, (LAST_LOOP + 1 - FIRST_LOOP) // 2) as i:
                iteration(i + FIRST_LOOP // 2, 1)
                iteration(i + (FIRST_LOOP + 1) // 2, 0)
            for c in range(LAST_LOOP + 1, NC + 3):
                iteration(c // 2, c % 2)

        def need(eng, semaphore, count):
            if not isinstance(count, int) or count > 0:
                eng.wait_ge(semaphore, count)

        def of_parity(h, p, lag):
            return h + (p - lag) // 2 + 1

        block = ctx.enter_context(nc.Block())

        @block.sync
        def _(sp):
            sp.dma_start(gru[:, 0:G_W], gru_pack[:, 0:G_W]).then_inc(s_cond_w, 16)
            sp.dma_start(xin[0][:, :], x_t[:, 0:CB]).then_inc(x_loaded[0], 16)
            sp.dma_start(gru[:, G_W:G_END], gru_pack[:, G_W:G_END]).then_inc(s_gru, 16)
            sp.dma_start(rnn[1][:, cols(ST - 1)], gru_pack[:, 0:B]).then_inc(s_h30, 16)
            sp.dma_start(xin[1][:, :], x_t[:, CB:2 * CB]).then_inc(x_loaded[1], 16)
            sp.dma_start(ada[:, :], ada_pack).then_inc(s_ada, 16)
            for m in range(4):
                sp.dma_start(w2[:, m], w2_pack[:, m]).then_inc(s_w2[m], 16)
            sp.dma_start(moe[:, :], moe_pack).then_inc(s_moe, 16)

            def iteration(h, p):
                c = 2 * h + p
                if has(c, -1) and not (isinstance(c, int) and c == 0):
                    sp.wait_ge(x0_ready, c)
                    sp.dma_start(xin[1 - p][:, :], x_t[:, bass.ds(c * CB + CB, CB)]).then_inc(x_loaded[1 - p], 16)
                if has(c, 3):
                    sp.wait_ge(y_ready, c - 2)
                    sp.dma_start(out_t[:, bass.ds((c - 3) * CB, CB)], yout[1 - p][:, :]).then_inc(y_stored[1 - p], 16)

            run_iterations(iteration, sp)
            for p in range(2):
                sp.wait_ge(y_stored[p], 16 * (NC // 2))

        @block.gpsimd
        def _(pool):
            pool.memset(ones[:, :], 1.0).then_inc(s_ones, 1)
            pool.memset(hist[1][:, cols(ST - 1)], 0.0).then_inc(h_zero, 1)
            pool.memset(lnstat[:, 5:6], -0.5).then_inc(s_half, 1)
            pool.memset(euler[:, :], EULER).then_inc(s_half, 1)
            pool.memset(ones_wide[:, :], 1.0).then_inc(s_half, 1)
            pool.wait_ge(s_gru, 16)
            pool.tensor_scalar(u_scaled[:, 0:2 * D], gru[:, G_U:G_U + 2 * D], 0.5, None, ALU.mult).then_inc(u_ready, 1)
            pool.tensor_scalar(u_scaled[:, 2 * D:3 * D], gru[:, G_U + 2 * D:G_END], 0.25, None,
                               ALU.mult).then_inc(u_ready, 1)
            pool.wait_ge(s_const, 16)
            pool.tensor_copy(hot[:, :], const[0:96, K_HOT:K_HOT + CB]).then_inc(s_hot, 1)
            pool.wait_ge(ln_dve, LN_VAR)
            pool.wait_ge(s_half, 3)
            pool.tensor_tensor(lnstat[:, 4:5], lnstat[:, 3:4], lnstat[:, 5:6], ALU.pow).then_inc(ln_pow, 1)

            def iteration(h, p):
                c = 2 * h + p
                if has(c, 1):
                    pool.wait_ge(neg_ready, c)
                    pool.tensor_tensor(expneg[:, 0, :], euler[:, :], neglog[:, :], ALU.pow).then_inc(exp_ready, 1)
                    pool.wait_ge(exp_ready, c)
                    pool.tensor_tensor(expneg[:, 1, :], expneg[:, 0, :], ones_wide[:, :], ALU.add).then_inc(sum_ready, 1)
                if has(c, 3):
                    pool.wait_ge(x2_ready, c - 2)
                    pool.wait_ge(n_ready, c * ST - 2 * ST)
                    need(pool, y_stored[1 - p], 16 * of_parity(h, p, 5))
                    pool.tensor_tensor(yout[1 - p][:, :], x2[1 - p][:, :], rnn[1 - p][:, :],
                                       ALU.add).then_inc(y_ready, 1)

            run_iterations(iteration, pool)

        @block.tensor
        def _(pe):
            mm = nc.tensor.matmul

            pe.wait_ge(s_cond_w, 16)
            mm(ps_b[0:96, 0:V_B], gru[:, G_COND:G_COND + 96], gru[:, G_C:G_C + V_B], start=True, stop=False)
            pe.wait_ge(s_ones, 1)
            pe.wait_ge(s_rows, 16)
            mm(ps_b[0:96, 0:V_B], ones[:, :], rows[:, 0:V_B], start=False, stop=True)
            mm(ps_c[0:96, 0:V_END - V_B], ones[:, :], rows[:, V_B:V_END], start=True, stop=True).then_inc(v_mm, 1)

            def project(out, v, w, src, first, inc=None):
                mm(out, vparts[:, v:v + 128], hot[:, :], start=first, stop=False, skip_group_check=True)
                mm(out, w, src, start=False, stop=True, skip_group_check=True)

            def gate_w(n):
                return gru[:, G_W + n * 128:G_W + (n + 1) * 128]

            def gate_u(n):
                return u_scaled[:, n * 128:(n + 1) * 128]

            def project_z(h, p):
                pe.wait_ge(x_loaded[1 - p], 16 * of_parity(h, p, -1))
                project(ps_z[1 - p][:, 0:CB], V_Z, gate_w(1), xin[1 - p][:, :], True)

            def project_r(p):
                project(ps_rh[1 - p][:, 0:CB], V_R, gate_w(0), xin[1 - p][:, :], True)

            def project_h(p):
                project(ps_rh[1 - p][:, CB:2 * CB], V_H, gate_w(2), xin[1 - p][:, :], False)

            def adapter_mm(i):
                m, bank_m = i // 2, (ps_a, ps_b, ps_c, ps_a)[i // 2]
                if i == 0:
                    pe.wait_ge(h2_ready, 1)
                if i % 2 == 0:
                    pe.wait_ge(s_w2[m], 16)
                if i == 6:
                    pe.wait_ge(w_out, 1)
                for r in range(4 * (i % 2), 4 * (i % 2) + 4):
                    last = mm(bank_m[:, r * B:(r + 1) * B], w2[:, m, r, :], adah[:, 3, :], start=True, stop=True)
                if i % 2:
                    last.then_inc(w_mm, 1)

            def setup(c, s, slot):
                if (c, s, slot) == (0, 1, 0):
                    pe.wait_ge(ln_dve, LN_OUT)
                    pe.wait_ge(s_const, 16)
                    pe.wait_ge(v_ready, 1)
                    nc.tensor.transpose(ps_b[:, 0:B], lnbuf[:, 3, :], ident[0:B, 0:B]).then_inc(ln_tp, 1)
                if (c, s, slot) == (0, 2, 0):
                    pe.wait_ge(c_ready, 1)
                    pe.wait_ge(s_ada, 16)
                    mm(ps_c[:, 0:B], ada[:, A_W1:A_W1 + D], adah[:, 0, :], start=True, stop=True).then_inc(h2_mm, 1)
                if c == 0 and s >= 4:
                    adapter_mm(2 * (s - 4) + slot)
                if (c, s, slot) == (1, 0, 0):
                    pe.wait_ge(w_out, 4)
                    for k, m in enumerate((A1, B2)):
                        for g in range(2):
                            last = nc.tensor.transpose(ps_a[:, (2 * k + g) * 128:(2 * k + g + 1) * 128],
                                                       adapt[:, m, g * GB:(g + 1) * GB, :], ident)
                    last.then_inc(t_mm, 1)

            def group(t, g):
                return t.rearrange("p (t b) -> p t b", b=B)[:, :, g * GB:(g + 1) * GB]

            def down_and_u(c):
                pe.wait_ge(x1_ready, c - 1)
                mm(ps_a[:, 0:CB], ada[:, A_DOWN:A_DOWN + D], x1[:, :], start=True, stop=False, skip_group_check=True)
                for g in range(2):
                    last = mm(ps_a[:, CB + g * 128:CB + (g + 1) * 128], adapt[:, A2, g * GB:(g + 1) * GB, :],
                              group(x1[:, :], g), start=False, stop=True, skip_group_check=True)
                last.then_inc(down_mm, 1)

            def add_low_rank(c, masked, count, k, done):
                pe.wait_ge(masked, c - 1)
                for g in range(2):
                    last = mm(group(ps_a[:, 0:CB], g), adapt_t[:, k, g, :], proj[:, g], start=False, stop=True,
                              skip_group_check=True)
                last.then_inc(done, 1)

            def up_and_v(c):
                pe.wait_ge(mid_ready, c - 1)
                mm(ps_a[:, 0:CB], ada[:, A_UP:A_UP + D], mid[:, :], start=True, stop=False, skip_group_check=True)
                for g in range(2):
                    last = mm(ps_a[:, CB + g * 128:CB + (g + 1) * 128], adapt[:, B1, g * GB:(g + 1) * GB, :],
                              group(mid[:, :], g), start=False, stop=True, skip_group_check=True)
                last.then_inc(up_mm, 1)

            def router(c, p):
                pe.wait_ge(x0_ready, c)
                if isinstance(c, int) and c == 1:
                    pe.wait_ge(s_moe, 16)
                for k in range(2):
                    tile = slice(k * 128, (k + 1) * 128)
                    mm(ps_b[:, k * NE:(k + 1) * NE], x0[1 - p][:, tile], moe[:, M_RT:M_RT + NE],
                       start=True, stop=False)
                    last = mm(ps_b[:, k * NE:(k + 1) * NE], hot[:, tile], vparts[:, V_T:V_T + NE],
                              start=False, stop=True)
                last.then_inc(router_mm, 1)

            def up_product(out, col, k, src):
                return mm(out[:, k * CB:(k + 1) * CB], moe[:, col + k * 128:col + (k + 1) * 128], src[:, :],
                          start=True, stop=True)

            def experts_up(c, p, k):
                out = (ps_c, ps_b)[k // 2]
                last = mm(out[:, (k % 2) * CB:(k % 2 + 1) * CB], moe[:, M_RW1 + k * 128:M_RW1 + (k + 1) * 128],
                          x0[1 - p][:, :], start=True, stop=True)
                if k % 2:
                    last.then_inc(rw1_mm, 1)

            def gates_by_row(half):
                out, wide = (ps_c, ps_b)[half], gates_wide[half]
                for k in range(2):
                    for tile in range(2):
                        last = nc.tensor.transpose(
                            out[:, k * CB + tile * 128:k * CB + (tile + 1) * 128],
                            wide[:, tile, 2 * k:2 * k + 2, :], ident)
                last.then_inc(gate_tp, 1)

            def moe_down(k):
                col, src = (M_SW2 + k * 128, shared[:, k, :]) if k < 2 else (M_RW2 + (k - 2) * 128, hid[:, k - 2, :])
                last = mm(ps_a[:, 0:CB], moe[:, col:col + 128], src, start=(k == 0), stop=(k == 5))
                if k == 5:
                    last.then_inc(moe_mm, 1)

            def slot_a(h, p, c, s):
                if isinstance(c, int):
                    setup(c, s, 0)
                if s == 1 and has(c, -1):
                    project_z(h, p)
                if has(c, 1):
                    if s == 0:
                        router(c, p)
                    if s == 2:
                        up_product(ps_c, M_SW1, 1, x0[1 - p]).then_inc(sw1_mm, 1)
                    if s == 4:
                        experts_up(c, p, 1)
                    if s == 5:
                        pe.wait_ge(shared_ready, c)
                        experts_up(c, p, 2)
                    if s == 6:
                        pe.wait_ge(wide_ready, 2 * c - 1)
                        pe.wait_ge(gelu_ready, 2 * c - 1)
                        gates_by_row(0)
                        need(pe, x2_ready, c - 1)
                        moe_down(0)
                    if s == 7:
                        pe.wait_ge(wide_ready, 2 * c)
                        pe.wait_ge(gelu_ready, 2 * c)
                        gates_by_row(1)
                        pe.wait_ge(hid_ready, 2 * c - 1)
                        moe_down(2)
                if s == 3 and has(c, 2):
                    up_and_v(c)

            def slot_b(h, p, c, s):
                if isinstance(c, int):
                    setup(c, s, 1)
                if s == 0 and has(c, 2):
                    down_and_u(c)
                if s == 1 and has(c, 2):
                    add_low_rank(c, um_ready, 1, 1, pre_mm)
                if s == 4 and has(c, 2):
                    add_low_rank(c, vm_ready, 1, 0, ada_mm)
                if has(c, 1):
                    if s == 1:
                        up_product(ps_c, M_SW1, 0, x0[1 - p])
                    if s == 2:
                        pe.wait_ge(neg_ready, c)
                        up_product(ps_b, M_SW1 + HS, 0, x0[1 - p])
                        up_product(ps_b, M_SW1 + HS, 1, x0[1 - p]).then_inc(sw3_mm, 1)
                    if s == 3:
                        pe.wait_ge(sa_ready, c)
                        experts_up(c, p, 0)
                    if s == 5:
                        experts_up(c, p, 3)
                    if s == 6:
                        moe_down(1)
                    if s == 7:
                        moe_down(3)
                        pe.wait_ge(hid_ready, 2 * c)
                        moe_down(4)
                        moe_down(5)
                if has(c, -1):
                    if s == 4:
                        project_r(p)
                    if s == 6:
                        project_h(p)
                if s == ST - RNN_EARLY and has(c, 2):
                    pe.wait_ge(x2_ready, c - 1)
                    need(pe, n_ready, c * ST - 2 * ST)
                    project(ps_n[:, 0:CB], V_B, ada[:, A_WX:A_WX + D], x2[p][:, :], True)
                if has(c, 3 if s < ST - RNN_EARLY else 2):
                    k = (s + RNN_EARLY) % ST
                    q = p if s >= ST - RNN_EARLY else 1 - p
                    before = rnn[q][:, cols(k - 1)] if k else rnn[1 - q][:, cols(ST - 1)]
                    need(pe, n_ready, RNN_STEP(c, s))
                    if isinstance(c, int) and RNN_STEP(c, s) == 0:
                        pe.wait_ge(s_h30, 16)
                    mm(ps_n[:, cols(k)], ada[:, A_WH:A_WH + D], before, start=False, stop=True,
                       skip_group_check=True).then_inc(n_mm, 1)

            pe.wait_ge(v_ready, 1)
            pe.wait_ge(s_hot, 1)
            pe.wait_ge(s_gru, 16)
            project_z(-1, 1)
            project_r(1)
            project_h(1)

            def iteration(h, p):
                c = 2 * h + p
                for s in range(ST):
                    before = hist[p][:, cols(s - 1)] if s else hist[1 - p][:, cols(ST - 1)]
                    if has(c, 0):
                        if isinstance(c, int) and c * ST + s == 0:
                            pe.wait_ge(h_zero, 1)
                            pe.wait_ge(u_ready, 2)
                        need(pe, h_ready, c * ST + s)
                        mm(ps_rh[p][:, cols(s)], gate_u(0), before, start=False, stop=True,
                           skip_group_check=True).then_inc(r_mm, 1)
                        mm(ps_z[p][:, cols(s)], gate_u(1), before, start=False, stop=True,
                           skip_group_check=True).then_inc(z_mm, 1)
                    slot_a(h, p, c, s)
                    if has(c, 0):
                        pe.wait_ge(rh_ready, c * ST + s + 1)
                        mm(ps_rh[p][:, CB + s * B:CB + (s + 1) * B], gate_u(2), rh[:, :], start=False, stop=True,
                           skip_group_check=True).then_inc(c_mm, 1)
                    slot_b(h, p, c, s)

            run_iterations(iteration, pe)

        @block.scalar
        def _(act):
            act.dma_start(const[:, :], const_pack).then_inc(s_const, 16)
            act.dma_start(rows[:, :], add_rows).then_inc(s_rows, 16)
            act.dma_start(cond[:, :], cond_nat).then_inc(s_cond, 16)
            fn = nc.scalar.activation
            act.wait_ge(s_ones, 1)
            fn(table_load[:, :], ones[:, 0:1], ACT.Gelu)

            def slot_a(c, p, s):
                if isinstance(c, int) and (c, s) == (0, 3):
                    act.wait_ge(h2_mm, 1)
                    fn(adah[:, 3, :], ps_c[:, 0:B], ACT.Gelu, bias=ada[:, A_BIAS1:A_BIAS1 + 1]).then_inc(h2_ready, 1)
                if s == 2 and has(c, 2):
                    act.wait_ge(pre_mm, c - 1)
                    fn(mid[:, :], ps_a[:, 0:CB], ACT.Gelu).then_inc(mid_ready, 1)
                if s in (4, 5) and has(c, 1):
                    half = s - 4
                    act.wait_ge(gates_ready, c)
                    fn(gates_wide[half][:, :, :, :], gates[:, :, 4 * half:4 * half + 4].unsqueeze(3).broadcast_to(
                        [128, 2, NE // 2, HR]), ACT.Copy).then_inc(wide_ready, 1)
                if s == 6 and has(c, 1):
                    act.wait_ge(rw1_mm, 2 * c)
                    fn(hid[:, 2:4, :], ps_b[:, :].rearrange("p (k n) -> p k n", k=2), ACT.Gelu).then_inc(gelu_ready, 1)

            def slot_b(c, p, s):
                if has(c, 1):
                    if s == 2:
                        act.wait_ge(sw1_mm, c)
                        fn(shared[:, :, :], ps_c[:, :].rearrange("p (k n) -> p k n", k=2),
                           ACT.Tanh, scale=0.5).then_inc(sig_ready, 1)
                    if s == 4:
                        act.wait_ge(rw1_mm, 2 * c - 1)
                        fn(hid[:, 0:2, :], ps_c[:, :].rearrange("p (k n) -> p k n", k=2), ACT.Gelu).then_inc(gelu_ready, 1)

            def iteration(h, p):
                c = 2 * h + p
                for s in range(ST):
                    if has(c, 0):
                        act.wait_ge(r_mm, c * ST + s + 1)
                        fn(rgate[:, :], ps_rh[p][:, cols(s)], ACT.Tanh, scale=0.5).then_inc(r_ready, 1)
                        act.wait_ge(z_mm, c * ST + s + 1)
                        fn(zgate[:, :], ps_z[p][:, cols(s)], ACT.Tanh, scale=0.5).then_inc(z_ready, 1)
                    slot_a(c, p, s)
                    if has(c, 0):
                        act.wait_ge(c_mm, c * ST + s + 1)
                        fn(cand[:, :], ps_rh[p][:, CB + s * B:CB + (s + 1) * B], ACT.Tanh).then_inc(cand_ready, 1)
                    if has(c, 3 if s < ST - RNN_EARLY else 2):
                        k = (s + RNN_EARLY) % ST
                        q = p if s >= ST - RNN_EARLY else 1 - p
                        if k == 0:
                            need(act, y_ready, c - 3)
                        act.wait_ge(n_mm, RNN_STEP(c, s) + 1)
                        fn(rnn[q][:, cols(k)], ps_n[:, cols(k)], ACT.Tanh).then_inc(n_ready, 1)
                    slot_b(c, p, s)

            run_iterations(iteration, act)

        @block.vector
        def _(dve):
            v = nc.vector
            links = [0]

            def link(ins):
                links[0] += 1
                ins.then_inc(setup_chain, 1)
                dve.wait_ge(setup_chain, links[0])

            dve.wait_ge(v_mm, 1)
            link(v.tensor_copy(vres[:, 0:V_B], ps_b[0:96, 0:V_B]))
            link(v.tensor_copy(vres[:, V_B:V_END], ps_c[0:96, 0:V_END - V_B]))
            v.tensor_copy(vparts[0:32, :], vres[0:32, :])
            link(v.tensor_copy(vtop[32:64, :], vres[32:64, :]))
            link(v.tensor_copy(vtop[64:96, :], vres[64:96, :]))
            link(v.tensor_tensor(vres[32:64, :], vres[32:64, :], vtop[32:64, :], ALU.subtract))
            link(v.tensor_tensor(vres[64:96, :], vres[64:96, :], vtop[64:96, :], ALU.subtract))
            v.tensor_copy(vparts[32:64, :], vres[32:64, :])
            link(v.tensor_copy(vtop2[64:96, :], vres[64:96, :]))
            v.tensor_tensor(vparts[64:96, :], vres[64:96, :], vtop2[64:96, :], ALU.subtract).then_inc(v_ready, 1)

            dve.wait_ge(s_cond, 16)
            ln_count = [0]

            def ln(ins):
                ln_count[0] += 1
                ins.then_inc(ln_dve, 1)
                dve.wait_ge(ln_dve, ln_count[0])

            ln(v.reduce_sum(lnstat[:, 0:1], cond[:, :], axis=AX.X))
            ln(v.tensor_scalar(lnstat[:, 1:2], lnstat[:, 0:1], -1.0 / D, None, ALU.mult))
            ln(v.tensor_scalar(lnbuf[:, 0, :], cond[:, :], lnstat[:, 1:2], None, ALU.add))
            ln(v.tensor_tensor(lnbuf[:, 1, :], lnbuf[:, 0, :], lnbuf[:, 0, :], ALU.mult))
            ln(v.reduce_sum(lnstat[:, 2:3], lnbuf[:, 1, :], axis=AX.X))
            ln(v.tensor_scalar(lnstat[:, 3:4], lnstat[:, 2:3], 1.0 / D, LN_EPS, ALU.mult, ALU.add))
            assert ln_count[0] == LN_VAR
            dve.wait_ge(ln_pow, 1)
            ln(v.tensor_scalar(lnbuf[:, 3, :], lnbuf[:, 0, :], lnstat[:, 4:5], None, ALU.mult))
            assert ln_count[0] == LN_OUT

            def setup(c, s, slot):
                if (c, s, slot) == (0, 1, 1):
                    dve.wait_ge(ln_tp, 1)
                    dve.wait_ge(s_ada, 16)
                    v.tensor_scalar(adah[:, 0, :], ps_b[:, 0:B], ada[:, A_GAMMA:A_GAMMA + 1],
                                    ada[:, A_BETA:A_BETA + 1], ALU.mult, ALU.add).then_inc(c_ready, 1)
                if c == 0 and s >= 4 and slot:
                    m = s - 4
                    dve.wait_ge(w_mm, m + 1)
                    out = adapt[:, m].rearrange("p b r -> p r b")
                    bias = ada[:, A_BIAS2 + m * R:A_BIAS2 + (m + 1) * R].unsqueeze(2).broadcast_to([128, R, B])
                    v.tensor_tensor(out, (ps_a, ps_b, ps_c, ps_a)[m][:, 0:CB].rearrange("p (r b) -> p r b", b=B),
                                    bias, ALU.add).then_inc(w_out, 1)
                if (c, s, slot) == (1, 0, 0):
                    dve.wait_ge(t_mm, 1)
                    v.tensor_copy(adapt_t[:, :, :, :].rearrange("p k g n -> p (k g n)"), ps_a[:, :]).then_inc(t_out, 1)

            def masked(c, done, out_sem):
                dve.wait_ge(done, c - 1)
                v.tensor_tensor(proj[:, :, :, :].rearrange("p g t b -> p (g t) b"),
                                ps_a[:, CB:2 * CB].rearrange("p (n b) -> p n b", b=GB),
                                mask.unsqueeze(1).broadcast_to([128, 2 * ST, GB]), ALU.mult).then_inc(out_sem, 1)

            def gate_steps(c, steps):
                score, biased, rank = sel[:, 0], sel[:, 1], sel[:, 2]
                by_e = biased.unsqueeze(3).broadcast_to([128, 2, NE, NE])
                by_j = biased.unsqueeze(2).broadcast_to([128, 2, NE, NE])
                above, at_least, beats = pair[:, 0], pair[:, 1], pair[:, 2]
                chosen, picked, t1, t2 = gmask[:, 0], gmask[:, 1], gmask[:, 2], gmask[:, 3]
                den, den_eps, rden, ok, scale, other = (gst[:, n] for n in range(6))
                wide = lambda a: a.unsqueeze(2).broadcast_to([128, 2, NE])
                for n in steps:
                    if n == 0:
                        dve.wait_ge(sum_ready, c)
                        ins = v.reciprocal(score, expneg[:, 1, :].rearrange("p (k e) -> p k e", k=2))
                    if n > 0:
                        dve.wait_ge(gate_chain, (c - 1) * (GATE_STEPS - 1) + n)
                    if n == 1:
                        ins = v.tensor_tensor(biased, score, moe[:, M_RB:M_RB + 2 * NE].rearrange(
                            "p (k e) -> p k e", k=2), ALU.add)
                    if n == 2:
                        ins = v.tensor_tensor(at_least, by_j, by_e, ALU.is_ge)
                    if n == 3:
                        ins = v.tensor_tensor(above, by_j, by_e, ALU.is_gt)
                    if n == 4:
                        ins = v.tensor_tensor(at_least, at_least, lt.unsqueeze(1).broadcast_to([128, 2, NE, NE]),
                                              ALU.mult)
                    if n == 5:
                        ins = v.tensor_tensor(beats, above, at_least, ALU.max)
                    if n == 6:
                        ins = v.reduce_sum(rank, beats, axis=AX.X)
                    if n == 7:
                        ins = v.tensor_scalar(chosen, rank, 2.0, None, ALU.is_lt)
                    if n == 8:
                        ins = v.tensor_tensor(picked, chosen, score, ALU.mult)
                    if n == 9:
                        ins = v.reduce_sum(den, picked, axis=AX.X)
                    if n == 10:
                        ins = v.tensor_scalar(den_eps, den, ROUTER_EPS, None, ALU.add)
                    if n == 11:
                        ins = v.reciprocal(rden, den_eps)
                    if n == 12:
                        ins = v.tensor_scalar(ok, den, ROUTER_EPS, 2.0, ALU.is_gt, ALU.mult)
                    if n == 13:
                        ins = v.tensor_tensor(scale, ok, rden, ALU.mult)
                    if n == 14:
                        ins = v.tensor_scalar(other, ok, -0.5, 1.0, ALU.mult, ALU.add)
                    if n == 15:
                        ins = v.tensor_tensor(t1, picked, wide(scale), ALU.mult)
                    if n == 16:
                        ins = v.tensor_tensor(t2, chosen, wide(other), ALU.mult)
                    if n == 17:
                        v.tensor_tensor(gates[:, :, :], t1, t2, ALU.add).then_inc(gates_ready, 1)
                    else:
                        ins.then_inc(gate_chain, 1)

            def flat(t):
                return t.rearrange("p k n -> p (k n)")

            def gate_half(c, half):
                dve.wait_ge(gate_tp, 2 * c - 1 + half)
                part = flat(hid[:, 2 * half:2 * half + 2, :])
                v.tensor_tensor(part, part, (ps_c, ps_b)[half][:, :], ALU.mult).then_inc(hid_ready, 1)

            def slot_a(c, p, s):
                if isinstance(c, int):
                    setup(c, s, 0)
                if s == 0 and has(c, 2):
                    dve.wait_ge(moe_mm, c - 1)
                    v.scalar_tensor_tensor(x1[:, :], ps_a[:, 0:CB], 1.0 / 6.0, x0[p][:, :], ALU.mult,
                                           ALU.add).then_inc(x1_ready, 1)
                if has(c, 1):
                    if s == 0:
                        dve.wait_ge(router_mm, c)
                        v.tensor_scalar(neglog[:, :], ps_b[:, 0:2 * NE], -1.0, None, ALU.mult).then_inc(neg_ready, 1)
                    if s == 2:
                        gate_steps(c, range(5, 10))
                    if s == 3:
                        dve.wait_ge(sig_ready, c)
                        v.scalar_tensor_tensor(flat(shared[:, :, :]), flat(shared[:, :, :]), 1.0, ps_c[:, :],
                                               ALU.add, ALU.mult).then_inc(sa_ready, 1)
                    if s == 4:
                        dve.wait_ge(sw3_mm, c)
                        dve.wait_ge(sa_ready, c)
                        v.tensor_tensor(flat(shared[:, :, :]), flat(shared[:, :, :]), ps_b[:, :],
                                        ALU.mult).then_inc(shared_ready, 1)
                    if s == 6:
                        dve.wait_ge(gelu_ready, 2 * c - 1)
                        gate_half(c, 0)
                    if s == 7:
                        gate_half(c, 1)

            def slot_b(c, p, s):
                if isinstance(c, int):
                    setup(c, s, 1)
                if has(c, 2):
                    if s == 0:
                        masked(c, down_mm, um_ready)
                    if s == 3:
                        masked(c, up_mm, vm_ready)
                    if s == 4:
                        dve.wait_ge(ada_mm, c - 1)
                        need(dve, y_ready, c - 3)
                        v.scalar_tensor_tensor(x2[p][:, :], x1[:, :], 2.0, ps_a[:, 0:CB], ALU.mult,
                                               ALU.add).then_inc(x2_ready, 1)
                if has(c, 1):
                    if s == 1:
                        gate_steps(c, range(0, 5))
                    if s == 2:
                        gate_steps(c, range(10, 14))
                    if s == 3:
                        gate_steps(c, range(14, GATE_STEPS))
                if s == ST - 1 and has(c, 0):
                    dve.wait_ge(h_ready, c * ST + ST)
                    v.scalar_tensor_tensor(x0[p][:, :], hist[p][:, :], 0.5, xin[p][:, :], ALU.mult,
                                           ALU.add).then_inc(x0_ready, 1)

            def iteration(h, p):
                c = 2 * h + p
                for s in range(ST):
                    g = c * ST + s
                    before = hist[p][:, cols(s - 1)] if s else hist[1 - p][:, cols(ST - 1)]
                    if has(c, 0):
                        dve.wait_ge(r_ready, g + 1)
                        v.scalar_tensor_tensor(rh[:, :], rgate[:, :], 1.0, before, ALU.add,
                                               ALU.mult).then_inc(rh_ready, 1)
                        dve.wait_ge(z_ready, g + 1)
                        v.scalar_tensor_tensor(keep[:, :], zgate[:, :], 1.0, before, ALU.subtract,
                                               ALU.mult).then_inc(keep_ready, 1)
                    slot_a(c, p, s)
                    if has(c, 0):
                        dve.wait_ge(keep_ready, g + 1)
                        dve.wait_ge(cand_ready, g + 1)
                        v.scalar_tensor_tensor(take[:, :], zgate[:, :], 1.0, cand[:, :], ALU.add,
                                               ALU.mult).then_inc(take_ready, 1)
                        dve.wait_ge(take_ready, g + 1)
                        v.scalar_tensor_tensor(hist[p][:, cols(s)], keep[:, :], -0.5, take[:, :], ALU.mult,
                                               ALU.add).then_inc(h_ready, 1)
                    slot_b(c, p, s)

            run_iterations(iteration, dve)


_INPUTS = ["x_t", "gru_pack", "add_rows", "cond_nat", "moe_pack", "ada_pack", "w2_pack", "const_pack"]


def kernel(**inputs):
    import numpy as np
    import concourse.bacc as bacc
    from concourse import mybir as mb
    from concourse.bass_utils import run_bass_kernel_spmd

    a = {k: np.asarray(v) for k, v in inputs.items()}
    n = lambda layer, name: a[f"L{layer}_cond_{name}"]
    f32 = np.float32

    x_t = a["x"].transpose(2, 1, 0).reshape(D, T * B)
    cond_t = a["cond_1024"].T
    gru_pack = np.concatenate(
        [cond_t] * 3 + [n(0, "C_r"), n(0, "C_z"), n(0, "C"), n(1, "router_t_w").T,
                        n(0, "W_r"), n(0, "W_z"), n(0, "W"), n(0, "U_r"), n(0, "U_z"), n(0, "U")], axis=1)
    add_rows = np.concatenate([n(0, "b_r"), n(0, "b_z"), n(0, "b"), np.zeros(NE, f32), n(3, "b")])[None]
    moe_pack = np.concatenate(
        [n(1, "sw1").T, n(1, "sw3").T, n(1, "rw1").reshape(NE * HR, D).T,
         n(1, "sw2").T.reshape(2, 128, D).transpose(1, 0, 2).reshape(128, 2 * D),
         n(1, "rw2").transpose(0, 2, 1).reshape(NE // 2, 2 * HR, D).transpose(1, 0, 2).reshape(128, NE // 2 * D),
         n(1, "router_w").T, np.broadcast_to(np.tile(n(1, "router_bias"), 2), (128, 2 * NE))], axis=1)
    ada_pack = np.concatenate(
        [n(2, "base_down"), n(2, "base_up").T, n(2, "W1"), n(2, "ln_gamma")[:, None], n(2, "ln_beta")[:, None],
         n(2, "bias1")[:, None], n(2, "bias2").reshape(4, D, R).transpose(1, 0, 2).reshape(D, 4 * R),
         n(3, "Wx"), n(3, "Wh")], axis=1)
    w2_pack = n(2, "W2").reshape(D, 4, D, R).transpose(0, 1, 3, 2)

    hot = np.zeros((128, CB), f32)
    for part in range(3):
        hot[part * B:(part + 1) * B] = np.tile(np.eye(B, dtype=f32), (1, ST))
    mask = np.repeat(np.eye(GB, dtype=f32), R, axis=0)
    lower = np.tril(np.ones((NE, NE), f32), -1).reshape(1, NE * NE)
    const_pack = np.concatenate([np.eye(128, dtype=f32), hot, mask, np.broadcast_to(lower, (128, NE * NE))], axis=1)

    values = dict(x_t=x_t, gru_pack=gru_pack, add_rows=add_rows, cond_nat=a["cond_1024"], moe_pack=moe_pack,
                  ada_pack=ada_pack, w2_pack=w2_pack, const_pack=const_pack)
    nc = bacc.Bacc("TRN2", target_bir_lowering=False, num_devices=1)
    arrays, args = {}, []
    for name in _INPUTS:
        v = np.ascontiguousarray(values[name])
        arrays[name + "_dram"] = v
        args.append(nc.dram_tensor(name + "_dram", v.shape, mb.dt.from_np(v.dtype), kind="ExternalInput").ap())
    args.append(nc.dram_tensor("out_dram", (D, T * B), mb.dt.float32, kind="ExternalOutput").ap())
    recurrent_stack_kernel(nc, *args)
    r = run_bass_kernel_spmd(nc, [arrays], core_ids=[0])
    return np.ascontiguousarray(np.asarray(r.results[0]["out_dram"]).reshape(D, T, B).transpose(2, 1, 0))
```

```python
import concourse.bass as bass
from concourse import mybir
from contextlib import ExitStack

B, T, D = 32, 128, 128
NE, HR, HS = 8, 64, 256
R = 8
ST = 8
NC = T // ST
CB = ST * B
GB = 16
ROUTER_EPS = 1e-9
LN_EPS = 1e-5
EULER = 2.718281828459045

V_R, V_Z, V_H, V_T, V_B, V_END = 0, 128, 256, 384, 392, 520
G_COND = 0
G_C = 96
G_W = G_C + 392
G_U = G_W + 384
G_END = G_U + 384
M_SW1, M_SW3, M_RW1, M_SW2, M_RW2, M_RT, M_RB = 0, 256, 512, 1024, 1280, 1792, 1800
M_END = M_RB + 16
A_DOWN, A_UP, A_W1, A_GAMMA, A_BETA, A_BIAS1, A_BIAS2, A_WX, A_WH = 0, 128, 256, 384, 385, 386, 387, 419, 547
A_END = A_WH + 128
K_ID, K_HOT, K_MASK, K_LT = 0, 128, 128 + CB, 128 + CB + GB
K_END = K_LT + NE * NE
A1, B1, A2, B2 = range(4)


def recurrent_stack_kernel(nc, x_t, gru_pack, add_rows, cond_nat, moe_pack, ada_pack, w2_pack, const_pack, out_t):
    f32, bf16, f32r = mybir.dt.float32, mybir.dt.bfloat16, mybir.dt.float32r
    ALU, ACT, AX = mybir.AluOpType, mybir.ActivationFunctionType, mybir.AxisListType

    ctx = ExitStack()
    with ctx:
        def sb(name, shape, dt=f32):
            return ctx.enter_context(nc.sbuf_tensor(name, shape, dt))

        def bank(name):
            return ctx.enter_context(nc.psum_tensor(name, [128, 512], f32))

        def sem(name):
            return ctx.enter_context(nc.semaphore(name))

        gru = sb("gru", [128, G_END])
        rows = sb("rows", [96, V_END])
        cond = sb("cond", [B, D])
        moe = sb("moe", [128, M_END])
        ada = sb("ada", [128, A_END])
        w2 = sb("w2", [128, 4, R, D])
        const = sb("const", [128, K_END])
        ident = const[:, K_ID:K_ID + 128]
        hot = sb("hot", [96, CB], bf16)
        vparts = sb("vparts", [96, V_END], bf16)
        vres = sb("vres", [96, V_END])
        vtop = sb("vtop", [96, V_END], bf16)
        gate_hi, gate_lo = sb("gate_hi", [128, 3 * D], f32r), sb("gate_lo", [128, 3 * D], f32r)
        up_hi, up_lo = sb("up_hi", [128, M_SW2], f32r), sb("up_lo", [128, M_SW2], f32r)
        x_hi, x_lo = sb("x_hi", [128, CB], f32r), sb("x_lo", [128, CB], f32r)
        x0_hi, x0_lo = sb("x0_hi", [128, CB], f32r), sb("x0_lo", [128, CB], f32r)
        filler = sb("filler", [128, 256], bf16)
        adapt = sb("adapt", [128, 4, B, R])
        adapt_t = sb("adapt_t", [128, 2, 2, 128])
        u_scaled = sb("u_scaled", [128, 3 * D])
        table_load = sb("table_load", [1, 1])
        euler, ones_wide = sb("euler", [128, 2 * NE]), sb("ones_wide", [128, 2 * NE])
        neglog, expneg = sb("neglog", [128, 2 * NE]), sb("expneg", [128, 2, 2 * NE])
        lnbuf = sb("lnbuf", [B, 4, D])
        lnstat = sb("lnstat", [B, 8])
        adah = sb("adah", [128, 4, B])
        xin = [sb(f"xin{p}", [128, CB]) for p in range(2)]
        hist = [sb(f"hist{p}", [128, CB]) for p in range(2)]
        x0 = [sb(f"x0_{p}", [128, CB]) for p in range(2)]
        x1 = sb("x1", [128, CB])
        x2 = [sb(f"x2_{p}", [128, CB]) for p in range(2)]
        rnn = [sb(f"rnn{p}", [128, CB]) for p in range(2)]
        yout = [sb(f"yout{p}", [128, CB]) for p in range(2)]
        rgate, zgate, cand = sb("rgate", [128, B]), sb("zgate", [128, B]), sb("cand", [128, B])
        rh, keep, take = sb("rh", [128, B]), sb("keep", [128, B]), sb("take", [128, B])
        shared = sb("shared", [128, 2, CB])
        hid = sb("hid", [128, 4, CB])
        sel = sb("sel", [128, 3, 2, NE])
        pair = sb("pair", [128, 3, 2, NE, NE])
        gst = sb("gst", [128, 8, 2])
        gmask = sb("gmask", [128, 4, 2, NE])
        gates = sb("gates", [128, 2, NE])
        gates_wide = [sb(f"gates_wide{k}", [128, 2, NE // 2, HR]) for k in range(2)]
        proj = sb("proj", [128, 2, ST, GB])
        mid = sb("mid", [128, CB])

        ps_rh = [bank(f"ps_rh{p}") for p in range(2)]
        ps_z = [bank(f"ps_z{p}") for p in range(2)]
        ps_n = bank("ps_n")
        ps_a, ps_b, ps_c = bank("ps_a"), bank("ps_b"), bank("ps_c")

        s_cond_w, s_gru, s_rows, s_cond, s_moe, s_ada, s_const, s_h30 = (
            sem(n) for n in ("cond_weights_loaded", "gru_loaded", "rows_loaded", "cond_loaded", "moe_loaded",
                             "ada_loaded", "const_loaded", "rnn_start_loaded"))
        s_w2 = [sem(f"w2_loaded{m}") for m in range(4)]
        x_loaded = [sem(f"x_loaded{p}") for p in range(2)]
        y_stored = [sem(f"y_stored{p}") for p in range(2)]
        s_hot, h_zero, s_half = (sem(n) for n in ("hot_ready", "h_start_ready", "half_ready"))
        v_mm, setup_chain, v_ready = sem("v_matmul_done"), sem("setup_chain"), sem("v_parts_ready")
        v_mid_ready, gate_hi_ready, gate_lo_ready, up_hi_ready, up_lo_ready, s_fill = (sem(n) for n in (
            "v_middle_ready", "gate_w_high", "gate_w_low", "up_w_high_half", "up_w_low_half", "filler_ready"))
        ln_dve, ln_pow, ln_tp = sem("ln_dve"), sem("ln_rsqrt_done"), sem("ln_transposed")
        c_ready, h2_mm, h2_ready = (sem(n) for n in ("ln_out_ready", "ada_hidden_mm", "ada_hidden_ready"))
        w_mm, w_out, t_mm, t_out, u_ready = (sem(n) for n in (
            "adapter_mm", "adapter_ready", "adapter_transposed", "adapter_t_ready", "u_scaled_ready"))
        LN_VAR, LN_OUT = 6, 7
        r_mm, z_mm, c_mm = sem("reset_mm"), sem("update_mm"), sem("cand_mm")
        r_ready, z_ready, cand_ready = sem("reset_ready"), sem("update_ready"), sem("cand_ready")
        rh_ready, keep_ready, take_ready, h_ready = (sem(n) for n in (
            "reset_h_ready", "keep_ready", "take_ready", "h_ready"))
        n_mm, n_ready = sem("rnn_mm"), sem("rnn_ready")
        x_hi_ready, x_lo_ready, x0_hi_ready, x0_lo_ready = (sem(n) for n in ("x_high", "x_low", "x0_high", "x0_low"))
        x0_ready, router_mm, neg_ready, exp_ready, sum_ready, gate_chain, gates_ready = (sem(n) for n in (
            "x0_ready", "router_mm", "neg_logits_ready", "exp_ready", "exp_plus_one_ready", "gates_chain",
            "gates_ready"))
        sw1_mm, sw3_mm, sig_ready, sa_ready, shared_ready = (sem(n) for n in (
            "sw1_mm", "sw3_mm", "sigmoid_ready", "silu_ready", "shared_hidden_ready"))
        wide_ready = sem("gates_wide_half")
        rw1_mm, gelu_ready, gate_tp, hid_ready = (sem(n) for n in (
            "rw1_mm_half", "gelu_half", "gates_transposed_half", "hidden_half"))
        moe_mm, x1_ready = sem("moe_out_mm"), sem("x1_ready")
        u_mm, um_ready, pre_mm, mid_ready = (sem(n) for n in (
            "u_mm", "u_masked", "mid_pre_mm", "mid_ready"))
        v_product_mm, vm_ready, ada_mm, x2_ready, y_ready = (sem(n) for n in (
            "v_mm_done", "v_masked", "adapter_out_mm", "x2_ready", "y_ready"))

        mask = const[:, K_MASK:K_MASK + GB]
        lt = const[:, K_LT:K_LT + NE * NE].rearrange("p (e j) -> p e j", e=NE)

        def cols(s, n=1):
            return slice(s * B, (s + n) * B)

        def has(c, lag):
            return not isinstance(c, int) or 0 <= c - lag < NC

        FIRST_LOOP, LAST_LOOP = 5, 14
        WARM_START, WARM_SPLIT, WARM = 16, 24, ((2, 3), (0, 0))
        GATE_STEPS = 18
        RNN_EARLY = 3

        def RNN_STEP(c, s):
            return c * ST + (s + RNN_EARLY - 3 * ST)


        def run_iterations(iteration, eng):
            for c in range(FIRST_LOOP):
                iteration(c // 2, c % 2)
            with eng.Fori(0, (LAST_LOOP + 1 - FIRST_LOOP) // 2) as i:
                iteration(i + FIRST_LOOP // 2, 1)
                iteration(i + (FIRST_LOOP + 1) // 2, 0)
            for c in range(LAST_LOOP + 1, NC + 3):
                iteration(c // 2, c % 2)

        def need(eng, semaphore, count):
            if not isinstance(count, int) or count > 0:
                eng.wait_ge(semaphore, count)

        def of_parity(h, p, lag):
            return h + (p - lag) // 2 + 1

        block = ctx.enter_context(nc.Block())

        @block.sync
        def _(sp):
            sp.dma_start(gru[:, 0:G_W], gru_pack[:, 0:G_W]).then_inc(s_cond_w, 16)
            sp.dma_start(xin[0][:, :], x_t[:, 0:CB]).then_inc(x_loaded[0], 16)
            sp.dma_start(gru[:, G_W:G_END], gru_pack[:, G_W:G_END]).then_inc(s_gru, 16)
            sp.dma_start(xin[1][:, :], x_t[:, CB:2 * CB]).then_inc(x_loaded[1], 16)
            sp.dma_start(rnn[1][:, cols(ST - 1)], gru_pack[:, 0:B]).then_inc(s_h30, 16)
            sp.dma_start(ada[:, :], ada_pack).then_inc(s_ada, 16)
            for m in range(4):
                sp.dma_start(w2[:, m], w2_pack[:, m]).then_inc(s_w2[m], 16)
            sp.dma_start(moe[:, :], moe_pack).then_inc(s_moe, 16)

            def iteration(h, p):
                c = 2 * h + p
                if has(c, -1) and not (isinstance(c, int) and c == 0):
                    sp.wait_ge(x0_ready, c)
                    sp.dma_start(xin[1 - p][:, :], x_t[:, bass.ds(c * CB + CB, CB)]).then_inc(x_loaded[1 - p], 16)
                if has(c, 3):
                    sp.wait_ge(y_ready, c - 2)
                    sp.dma_start(out_t[:, bass.ds((c - 3) * CB, CB)], yout[1 - p][:, :]).then_inc(y_stored[1 - p], 16)

            run_iterations(iteration, sp)
            for p in range(2):
                sp.wait_ge(y_stored[p], 16 * (NC // 2))

        @block.gpsimd
        def _(pool):
            def low_x(k, p):
                pool.wait_ge(x_hi_ready, k + 1)
                pool.tensor_tensor(x_lo[:, :], xin[p][:, :], x_hi[:, :].bitcast(f32),
                                   ALU.subtract).then_inc(x_lo_ready, 1)

            pool.memset(filler[:, :], 0.0).then_inc(s_fill, 1)
            pool.memset(hist[1][:, cols(ST - 1)], 0.0).then_inc(h_zero, 1)
            pool.memset(lnstat[:, 5:6], -0.5).then_inc(s_half, 1)
            pool.memset(euler[:, :], EULER).then_inc(s_half, 1)
            pool.memset(ones_wide[:, :], 1.0).then_inc(s_half, 1)
            low_x(0, 0)
            pool.wait_ge(s_gru, 16)
            pool.tensor_scalar(u_scaled[:, 0:2 * D], gru[:, G_U:G_U + 2 * D], 0.5, None, ALU.mult).then_inc(u_ready, 1)
            pool.tensor_scalar(u_scaled[:, 2 * D:3 * D], gru[:, G_U + 2 * D:G_END], 0.25, None,
                               ALU.mult).then_inc(u_ready, 1)
            pool.wait_ge(ln_dve, LN_VAR)
            pool.wait_ge(s_half, 3)
            pool.tensor_tensor(lnstat[:, 4:5], lnstat[:, 3:4], lnstat[:, 5:6], ALU.pow).then_inc(ln_pow, 1)

            def iteration(h, p):
                c = 2 * h + p
                if has(c, 1):
                    pool.wait_ge(neg_ready, c)
                    pool.tensor_tensor(expneg[:, 0, :], euler[:, :], neglog[:, :], ALU.pow).then_inc(exp_ready, 1)
                    pool.wait_ge(exp_ready, c)
                    pool.tensor_tensor(expneg[:, 1, :], expneg[:, 0, :], ones_wide[:, :], ALU.add).then_inc(sum_ready, 1)
                if has(c, 0) and has(c, -1):
                    low_x(c + 1, 1 - p)
                if has(c, 3):
                    pool.wait_ge(x2_ready, c - 2)
                    pool.wait_ge(n_ready, c * ST - 2 * ST)
                    need(pool, y_stored[1 - p], 16 * of_parity(h, p, 5))
                    pool.tensor_tensor(yout[1 - p][:, :], x2[1 - p][:, :], rnn[1 - p][:, :],
                                       ALU.add).then_inc(y_ready, 1)

            run_iterations(iteration, pool)

        @block.tensor
        def _(pe):
            mm = nc.tensor.matmul

            def keep_warm(n):
                for _ in range(n):
                    mm(ps_n[:, 0:256], filler[:, 0:128], filler[:, :], start=True, stop=True)

            pe.wait_ge(s_fill, 1)
            keep_warm(WARM_START)
            pe.wait_ge(s_cond_w, 16)
            mm(ps_b[0:96, 0:V_B], gru[:, G_COND:G_COND + 96], gru[:, G_C:G_C + V_B], start=True,
               stop=True).then_inc(v_mm, 1)
            keep_warm(WARM_SPLIT)

            def high_products(out, w_hi, w_lo, s_hi, first):
                mm(out, w_hi, s_hi, start=first, stop=False, skip_group_check=True)
                mm(out, w_lo, s_hi, start=False, stop=False, skip_group_check=True)

            def low_product(out, w_hi, s_lo):
                return mm(out, w_hi, s_lo, start=False, stop=True, skip_group_check=True)

            def add_product(out, w_hi, w_lo, s_hi, s_lo, first):
                high_products(out, w_hi, w_lo, s_hi, first)
                return low_product(out, w_hi, s_lo)

            def project(out, v, n, first):
                w = slice(n * 128, (n + 1) * 128)
                mm(out, vparts[:, v:v + 128], hot[:, :], start=first, stop=False, skip_group_check=True)
                add_product(out, gate_hi[:, w], gate_lo[:, w], x_hi[:, :], x_lo[:, :], False)

            def gate_u(n):
                return u_scaled[:, n * 128:(n + 1) * 128]

            def project_r(c, p):
                pe.wait_ge(x_lo_ready, c + 2)
                project(ps_rh[1 - p][:, 0:CB], V_R, 0, True)

            def project_h(p):
                project(ps_rh[1 - p][:, CB:2 * CB], V_H, 2, False)

            def project_z(p):
                project(ps_z[1 - p][:, 0:CB], V_Z, 1, True)

            def adapter_mm(i):
                m, bank_m = i // 2, (ps_a, ps_b, ps_c, ps_a)[i // 2]
                if i == 0:
                    pe.wait_ge(h2_ready, 1)
                if i % 2 == 0:
                    pe.wait_ge(s_w2[m], 16)
                if i == 6:
                    pe.wait_ge(w_out, 1)
                for r in range(4 * (i % 2), 4 * (i % 2) + 4):
                    last = mm(bank_m[:, r * B:(r + 1) * B], w2[:, m, r, :], adah[:, 3, :], start=True, stop=True)
                if i % 2:
                    last.then_inc(w_mm, 1)

            def setup(c, s, slot):
                if c < 2:
                    keep_warm(WARM[c][slot])
                if (c, s, slot) == (0, 1, 0):
                    pe.wait_ge(ln_dve, LN_OUT)
                    pe.wait_ge(s_const, 16)
                    pe.wait_ge(v_ready, 2)
                    nc.tensor.transpose(ps_b[:, 0:B], lnbuf[:, 3, :], ident[0:B, 0:B]).then_inc(ln_tp, 1)
                if (c, s, slot) == (0, 2, 0):
                    pe.wait_ge(c_ready, 1)
                    pe.wait_ge(s_ada, 16)
                    mm(ps_c[:, 0:B], ada[:, A_W1:A_W1 + D], adah[:, 0, :], start=True, stop=True).then_inc(h2_mm, 1)
                if c == 0 and s >= 4:
                    adapter_mm(2 * (s - 4) + slot)
                if (c, s, slot) == (1, 0, 0):
                    pe.wait_ge(w_out, 4)
                    for k, m in enumerate((A1, B2)):
                        for g in range(2):
                            last = nc.tensor.transpose(ps_a[:, (2 * k + g) * 128:(2 * k + g + 1) * 128],
                                                       adapt[:, m, g * GB:(g + 1) * GB, :], ident)
                    last.then_inc(t_mm, 1)

            def group(t, g):
                return t.rearrange("p (t b) -> p t b", b=B)[:, :, g * GB:(g + 1) * GB]

            def down_product(c):
                pe.wait_ge(x1_ready, c - 1)
                mm(ps_a[:, 0:CB], ada[:, A_DOWN:A_DOWN + D], x1[:, :], start=True, stop=False, skip_group_check=True)

            def low_rank(part, src, done):
                for g in range(2):
                    last = mm(ps_a[:, CB + g * 128:CB + (g + 1) * 128], adapt[:, part, g * GB:(g + 1) * GB, :],
                              group(src[:, :], g), start=False, stop=True, skip_group_check=True)
                last.then_inc(done, 1)

            def u_product():
                low_rank(A2, x1, u_mm)

            def v_product():
                low_rank(B1, mid, v_product_mm)

            def add_low_rank(c, masked, k, done):
                pe.wait_ge(masked, c - 1)
                for g in range(2):
                    last = mm(group(ps_a[:, 0:CB], g), adapt_t[:, k, g, :], proj[:, g], start=False, stop=True,
                              skip_group_check=True)
                last.then_inc(done, 1)

            def up_product_of_mid(c):
                pe.wait_ge(mid_ready, c - 1)
                mm(ps_a[:, 0:CB], ada[:, A_UP:A_UP + D], mid[:, :], start=True, stop=False, skip_group_check=True)

            def router(c, p):
                pe.wait_ge(x0_ready, c)
                if isinstance(c, int) and c == 1:
                    pe.wait_ge(s_moe, 16)
                for k in range(2):
                    tile = slice(k * 128, (k + 1) * 128)
                    mm(ps_b[:, k * NE:(k + 1) * NE], x0[1 - p][:, tile], moe[:, M_RT:M_RT + NE],
                       start=True, stop=False)
                    last = mm(ps_b[:, k * NE:(k + 1) * NE], hot[:, tile], vparts[:, V_T:V_T + NE],
                              start=False, stop=True)
                last.then_inc(router_mm, 1)

            def up_product(out, part, k, high=True, low=True):
                w = slice(k * 128, (k + 1) * 128)
                out = out[:, part * CB:(part + 1) * CB]
                if high:
                    high_products(out, up_hi[:, w], up_lo[:, w], x0_hi[:, :], True)
                return low_product(out, up_hi[:, w], x0_lo[:, :]) if low else None

            def gates_by_row(half):
                out, wide = (ps_c, ps_b)[half], gates_wide[half]
                for k in range(2):
                    for tile in range(2):
                        last = nc.tensor.transpose(
                            out[:, k * CB + tile * 128:k * CB + (tile + 1) * 128],
                            wide[:, tile, 2 * k:2 * k + 2, :], ident)
                last.then_inc(gate_tp, 1)

            def moe_down(k, half):
                col, src = (M_SW2 + k * 128, shared[:, k]) if k < 2 else (M_RW2 + (k - 2) * 128, hid[:, k - 2])
                part = slice(half * 128, (half + 1) * 128)
                last = mm(ps_a[:, part], moe[:, col:col + 128], src[:, part], start=(k == 0 and half == 0),
                          stop=(k == 5), skip_group_check=True)
                if (k, half) == (5, 1):
                    last.then_inc(moe_mm, 1)

            def slot_a(h, p, c, s):
                if isinstance(c, int):
                    setup(c, s, 0)
                if has(c, 2):
                    if s == 0:
                        moe_down(5, 1)
                    if s == 1:
                        u_product()
                    if s == 3:
                        up_product_of_mid(c)
                if has(c, 1):
                    if s == 0:
                        router(c, p)
                    if s == 1:
                        pe.wait_ge(x0_lo_ready, c)
                        up_product(ps_c, 0, 0, high=False)
                    if s == 2:
                        pe.wait_ge(neg_ready, c)
                        up_product(ps_b, 0, 2)
                        up_product(ps_b, 1, 3).then_inc(sw3_mm, 1)
                    if s == 4:
                        pe.wait_ge(sa_ready, c)
                        up_product(ps_c, 0, 4)
                        up_product(ps_c, 1, 5).then_inc(rw1_mm, 1)
                    if s == 5:
                        pe.wait_ge(shared_ready, c)
                        up_product(ps_b, 0, 6)
                        up_product(ps_b, 1, 7).then_inc(rw1_mm, 1)
                    if s == 6:
                        pe.wait_ge(wide_ready, 2 * c - 1)
                        pe.wait_ge(gelu_ready, 2 * c - 1)
                        gates_by_row(0)
                        moe_down(0, 1)
                    if s == 7:
                        pe.wait_ge(hid_ready, 2 * c - 1)
                        moe_down(2, 0)
                        moe_down(2, 1)
                        moe_down(3, 0)

            def slot_b(h, p, c, s):
                if isinstance(c, int):
                    setup(c, s, 1)
                if has(c, 1):
                    if s == 0:
                        if isinstance(c, int) and c == 1:
                            pe.wait_ge(up_lo_ready, 2)
                        pe.wait_ge(x0_hi_ready, c)
                        up_product(ps_c, 0, 0, low=False)
                    if s == 1:
                        up_product(ps_c, 1, 1).then_inc(sw1_mm, 1)
                    if s == 5:
                        need(pe, x2_ready, c - 1)
                        moe_down(0, 0)
                    if s == 6:
                        moe_down(1, 0)
                        moe_down(1, 1)
                        pe.wait_ge(wide_ready, 2 * c)
                        pe.wait_ge(gelu_ready, 2 * c)
                        gates_by_row(1)
                    if s == 7:
                        moe_down(3, 1)
                        pe.wait_ge(hid_ready, 2 * c)
                        moe_down(4, 0)
                        moe_down(4, 1)
                        moe_down(5, 0)
                if has(c, 2):
                    if s == 0:
                        down_product(c)
                    if s == 1:
                        add_low_rank(c, um_ready, 1, pre_mm)
                    if s == 3:
                        v_product()
                    if s == 4:
                        add_low_rank(c, vm_ready, 0, ada_mm)
                if has(c, -1):
                    if s == 2:
                        project_r(c, p)
                        project_h(p)
                    if s == 4:
                        project_z(p)
                if s == ST - RNN_EARLY and has(c, 2):
                    pe.wait_ge(x2_ready, c - 1)
                    need(pe, n_ready, c * ST - 2 * ST)
                    mm(ps_n[:, 0:CB], vparts[:, V_B:V_END], hot[:, :], start=True, stop=False, skip_group_check=True)
                    mm(ps_n[:, 0:CB], ada[:, A_WX:A_WX + D], x2[p][:, :], start=False, stop=True,
                       skip_group_check=True)
                if has(c, 3 if s < ST - RNN_EARLY else 2):
                    k = (s + RNN_EARLY) % ST
                    q = p if s >= ST - RNN_EARLY else 1 - p
                    before = rnn[q][:, cols(k - 1)] if k else rnn[1 - q][:, cols(ST - 1)]
                    need(pe, n_ready, RNN_STEP(c, s))
                    if isinstance(c, int) and RNN_STEP(c, s) == 0:
                        pe.wait_ge(s_h30, 16)
                    mm(ps_n[:, cols(k)], ada[:, A_WH:A_WH + D], before, start=False, stop=True,
                       skip_group_check=True).then_inc(n_mm, 1)

            pe.wait_ge(v_ready, 2)
            pe.wait_ge(s_hot, 1)
            pe.wait_ge(gate_lo_ready, 1)
            project_r(-1, 1)
            project_h(1)
            project_z(1)

            def iteration(h, p):
                c = 2 * h + p
                for s in range(ST):
                    before = hist[p][:, cols(s - 1)] if s else hist[1 - p][:, cols(ST - 1)]
                    if has(c, 0):
                        if isinstance(c, int) and c * ST + s == 0:
                            pe.wait_ge(h_zero, 1)
                            pe.wait_ge(u_ready, 2)
                        need(pe, h_ready, c * ST + s)
                        mm(ps_rh[p][:, cols(s)], gate_u(0), before, start=False, stop=True,
                           skip_group_check=True).then_inc(r_mm, 1)
                        mm(ps_z[p][:, cols(s)], gate_u(1), before, start=False, stop=True,
                           skip_group_check=True).then_inc(z_mm, 1)
                    slot_a(h, p, c, s)
                    if has(c, 0):
                        pe.wait_ge(rh_ready, c * ST + s + 1)
                        mm(ps_rh[p][:, CB + s * B:CB + (s + 1) * B], gate_u(2), rh[:, :], start=False, stop=True,
                           skip_group_check=True).then_inc(c_mm, 1)
                    slot_b(h, p, c, s)

            run_iterations(iteration, pe)

        @block.scalar
        def _(act):
            act.dma_start(const[:, :], const_pack).then_inc(s_const, 16)
            act.dma_start(rows[:, :], add_rows).then_inc(s_rows, 16)
            act.dma_start(cond[:, :], cond_nat).then_inc(s_cond, 16)
            fn = nc.scalar.activation
            act.wait_ge(s_fill, 1)
            fn(table_load[:, :], filler[0:1, 0:1], ACT.Gelu)
            act.wait_ge(x_loaded[0], 16)
            fn(x_hi[:, :], xin[0][:, :], ACT.Copy).then_inc(x_hi_ready, 1)
            act.wait_ge(s_const, 16)
            fn(hot[:, :], const[0:96, K_HOT:K_HOT + CB], ACT.Copy).then_inc(s_hot, 1)
            act.wait_ge(s_gru, 16)
            fn(gate_hi[:, :], gru[:, G_W:G_U], ACT.Copy).then_inc(gate_hi_ready, 1)
            act.wait_ge(v_mid_ready, 1)
            fn(vparts[32:64, :], vtop[32:64, :], ACT.Copy).then_inc(v_ready, 1)

            def slot_a(c, p, s):
                if s == 0 and has(c, 1):
                    act.wait_ge(x0_ready, c)
                    fn(x0_hi[:, :], x0[1 - p][:, :], ACT.Copy).then_inc(x0_hi_ready, 1)
                if isinstance(c, int) and c == 0 and s in (5, 6):
                    if s == 5:
                        act.wait_ge(s_moe, 16)
                    part = slice((s - 5) * 512, (s - 4) * 512)
                    fn(up_hi[:, part], moe[:, part], ACT.Copy).then_inc(up_hi_ready, 1)
                if isinstance(c, int) and (c, s) == (0, 3):
                    act.wait_ge(h2_mm, 1)
                    fn(adah[:, 3, :], ps_c[:, 0:B], ACT.Gelu, bias=ada[:, A_BIAS1:A_BIAS1 + 1]).then_inc(h2_ready, 1)
                if s == 2 and has(c, 2):
                    act.wait_ge(pre_mm, c - 1)
                    fn(mid[:, :], ps_a[:, 0:CB], ACT.Gelu).then_inc(mid_ready, 1)
                if s in (5, 6) and has(c, 1):
                    half = s - 5
                    act.wait_ge(gates_ready, c)
                    fn(gates_wide[half][:, :, :, :], gates[:, :, 4 * half:4 * half + 4].unsqueeze(3).broadcast_to(
                        [128, 2, NE // 2, HR]), ACT.Copy).then_inc(wide_ready, 1)
            def slot_b(h, c, p, s):
                if s == 1 and has(c, 0) and has(c, -1):
                    act.wait_ge(x_loaded[1 - p], 16 * of_parity(h, p, -1))
                    fn(x_hi[:, :], xin[1 - p][:, :], ACT.Copy).then_inc(x_hi_ready, 1)
                if has(c, 1):
                    if s == 2:
                        act.wait_ge(sw1_mm, c)
                        fn(shared[:, :, :], ps_c[:, :].rearrange("p (k n) -> p k n", k=2),
                           ACT.Tanh, scale=0.5).then_inc(sig_ready, 1)
                    if s in (4, 5):
                        half = s - 4
                        act.wait_ge(rw1_mm, 2 * c - 1 + half)
                        fn(hid[:, 2 * half:2 * half + 2, :], (ps_c, ps_b)[half][:, :].rearrange(
                            "p (k n) -> p k n", k=2), ACT.Gelu).then_inc(gelu_ready, 1)

            def iteration(h, p):
                c = 2 * h + p
                for s in range(ST):
                    if has(c, 0):
                        act.wait_ge(r_mm, c * ST + s + 1)
                        fn(rgate[:, :], ps_rh[p][:, cols(s)], ACT.Tanh, scale=0.5).then_inc(r_ready, 1)
                        act.wait_ge(z_mm, c * ST + s + 1)
                        fn(zgate[:, :], ps_z[p][:, cols(s)], ACT.Tanh, scale=0.5).then_inc(z_ready, 1)
                    slot_a(c, p, s)
                    if has(c, 0):
                        act.wait_ge(c_mm, c * ST + s + 1)
                        fn(cand[:, :], ps_rh[p][:, CB + s * B:CB + (s + 1) * B], ACT.Tanh).then_inc(cand_ready, 1)
                    if has(c, 3 if s < ST - RNN_EARLY else 2):
                        k = (s + RNN_EARLY) % ST
                        q = p if s >= ST - RNN_EARLY else 1 - p
                        if k == 0:
                            need(act, y_ready, c - 3)
                        act.wait_ge(n_mm, RNN_STEP(c, s) + 1)
                        fn(rnn[q][:, cols(k)], ps_n[:, cols(k)], ACT.Tanh).then_inc(n_ready, 1)
                    slot_b(h, c, p, s)

            run_iterations(iteration, act)

        @block.vector
        def _(dve):
            v = nc.vector
            links = [0]

            def link(ins):
                links[0] += 1
                ins.then_inc(setup_chain, 1)
                dve.wait_ge(setup_chain, links[0])

            dve.wait_ge(s_rows, 16)
            dve.wait_ge(v_mm, 1)
            link(v.tensor_tensor(rows[:, 0:V_B], ps_b[0:96, 0:V_B], rows[:, 0:V_B], ALU.add))
            link(v.tensor_copy(vparts[:, :], rows[:, :]))
            link(v.tensor_tensor(vres[:, :], rows[:, :], vparts[:, :], ALU.subtract))
            v.tensor_copy(vtop[:, :], vres[:, :]).then_inc(v_mid_ready, 1)
            dve.wait_ge(v_mid_ready, 1)
            v.tensor_tensor(vparts[64:96, :], vres[64:96, :], vtop[64:96, :], ALU.subtract).then_inc(v_ready, 1)
            dve.wait_ge(gate_hi_ready, 1)
            v.tensor_tensor(gate_lo[:, :], gru[:, G_W:G_U], gate_hi[:, :].bitcast(f32),
                            ALU.subtract).then_inc(gate_lo_ready, 1)

            dve.wait_ge(s_cond, 16)
            ln_count = [0]

            def ln(ins):
                ln_count[0] += 1
                ins.then_inc(ln_dve, 1)
                dve.wait_ge(ln_dve, ln_count[0])

            ln(v.reduce_sum(lnstat[:, 0:1], cond[:, :], axis=AX.X))
            ln(v.tensor_scalar(lnstat[:, 1:2], lnstat[:, 0:1], -1.0 / D, None, ALU.mult))
            ln(v.tensor_scalar(lnbuf[:, 0, :], cond[:, :], lnstat[:, 1:2], None, ALU.add))
            ln(v.tensor_tensor(lnbuf[:, 1, :], lnbuf[:, 0, :], lnbuf[:, 0, :], ALU.mult))
            ln(v.reduce_sum(lnstat[:, 2:3], lnbuf[:, 1, :], axis=AX.X))
            ln(v.tensor_scalar(lnstat[:, 3:4], lnstat[:, 2:3], 1.0 / D, LN_EPS, ALU.mult, ALU.add))
            assert ln_count[0] == LN_VAR
            dve.wait_ge(ln_pow, 1)
            ln(v.tensor_scalar(lnbuf[:, 3, :], lnbuf[:, 0, :], lnstat[:, 4:5], None, ALU.mult))
            assert ln_count[0] == LN_OUT

            def setup(c, s, slot):
                if c == 0 and s in (6, 7) and slot == 0:
                    part = slice((s - 6) * 512, (s - 5) * 512)
                    dve.wait_ge(up_hi_ready, s - 5)
                    v.tensor_tensor(up_lo[:, part], moe[:, part], up_hi[:, part].bitcast(f32),
                                    ALU.subtract).then_inc(up_lo_ready, 1)
                if (c, s, slot) == (0, 1, 1):
                    dve.wait_ge(ln_tp, 1)
                    dve.wait_ge(s_ada, 16)
                    v.tensor_scalar(adah[:, 0, :], ps_b[:, 0:B], ada[:, A_GAMMA:A_GAMMA + 1],
                                    ada[:, A_BETA:A_BETA + 1], ALU.mult, ALU.add).then_inc(c_ready, 1)
                if c == 0 and s >= 4 and slot:
                    m = s - 4
                    dve.wait_ge(w_mm, m + 1)
                    out = adapt[:, m].rearrange("p b r -> p r b")
                    bias = ada[:, A_BIAS2 + m * R:A_BIAS2 + (m + 1) * R].unsqueeze(2).broadcast_to([128, R, B])
                    v.tensor_tensor(out, (ps_a, ps_b, ps_c, ps_a)[m][:, 0:CB].rearrange("p (r b) -> p r b", b=B),
                                    bias, ALU.add).then_inc(w_out, 1)
                if (c, s, slot) == (1, 0, 0):
                    dve.wait_ge(t_mm, 1)
                    v.tensor_copy(adapt_t[:, :, :, :].rearrange("p k g n -> p (k g n)"), ps_a[:, :]).then_inc(t_out, 1)

            def masked(c, done, out_sem):
                dve.wait_ge(done, c - 1)
                v.tensor_tensor(proj[:, :, :, :].rearrange("p g t b -> p (g t) b"),
                                ps_a[:, CB:2 * CB].rearrange("p (n b) -> p n b", b=GB),
                                mask.unsqueeze(1).broadcast_to([128, 2 * ST, GB]), ALU.mult).then_inc(out_sem, 1)

            def gate_steps(c, steps):
                score, biased, rank = sel[:, 0], sel[:, 1], sel[:, 2]
                by_e = biased.unsqueeze(3).broadcast_to([128, 2, NE, NE])
                by_j = biased.unsqueeze(2).broadcast_to([128, 2, NE, NE])
                above, at_least, beats = pair[:, 0], pair[:, 1], pair[:, 2]
                chosen, picked, t1, t2 = gmask[:, 0], gmask[:, 1], gmask[:, 2], gmask[:, 3]
                den, den_eps, rden, ok, scale, other = (gst[:, n] for n in range(6))
                wide = lambda a: a.unsqueeze(2).broadcast_to([128, 2, NE])
                done = (c - 1) * (GATE_STEPS - 1)

                def after(n):
                    dve.wait_ge(gate_chain, done + n + 1)

                for n in steps:
                    if n == 0:
                        dve.wait_ge(sum_ready, c)
                        ins = v.reciprocal(score, expneg[:, 1, :].rearrange("p (k e) -> p k e", k=2))
                    if n == 1:
                        after(0)
                        ins = v.tensor_tensor(biased, score, moe[:, M_RB:M_RB + 2 * NE].rearrange(
                            "p (k e) -> p k e", k=2), ALU.add)
                    if n == 2:
                        after(1)
                        ins = v.tensor_tensor(at_least, by_j, by_e, ALU.is_ge)
                    if n == 3:
                        ins = v.tensor_tensor(above, by_j, by_e, ALU.is_gt)
                    if n == 4:
                        after(2)
                        ins = v.tensor_tensor(at_least, at_least, lt.unsqueeze(1).broadcast_to([128, 2, NE, NE]),
                                              ALU.mult)
                    if n == 5:
                        after(4)
                        ins = v.tensor_tensor(beats, above, at_least, ALU.max)
                    if n == 6:
                        after(5)
                        ins = v.reduce_sum(rank, beats, axis=AX.X)
                    if n == 7:
                        after(6)
                        ins = v.tensor_scalar(chosen, rank, 2.0, None, ALU.is_lt)
                    if n == 8:
                        after(7)
                        ins = v.tensor_tensor(picked, chosen, score, ALU.mult)
                    if n == 9:
                        after(8)
                        ins = v.reduce_sum(den, picked, axis=AX.X)
                    if n == 10:
                        after(9)
                        ins = v.tensor_scalar(ok, den, ROUTER_EPS, 2.0, ALU.is_gt, ALU.mult)
                    if n == 11:
                        ins = v.tensor_scalar(den_eps, den, ROUTER_EPS, None, ALU.add)
                    if n == 12:
                        after(11)
                        ins = v.reciprocal(rden, den_eps)
                    if n == 13:
                        ins = v.tensor_scalar(other, ok, -0.5, 1.0, ALU.mult, ALU.add)
                    if n == 14:
                        after(12)
                        ins = v.tensor_tensor(scale, ok, rden, ALU.mult)
                    if n == 15:
                        after(13)
                        ins = v.tensor_tensor(t2, chosen, wide(other), ALU.mult)
                    if n == 16:
                        after(14)
                        ins = v.tensor_tensor(t1, picked, wide(scale), ALU.mult)
                    if n == 17:
                        after(16)
                        v.tensor_tensor(gates[:, :, :], t1, t2, ALU.add).then_inc(gates_ready, 1)
                    else:
                        ins.then_inc(gate_chain, 1)

            def flat(t):
                return t.rearrange("p k n -> p (k n)")

            def gate_half(c, half):
                dve.wait_ge(gate_tp, 2 * c - 1 + half)
                part = flat(hid[:, 2 * half:2 * half + 2, :])
                v.tensor_tensor(part, part, (ps_c, ps_b)[half][:, :], ALU.mult).then_inc(hid_ready, 1)

            def slot_a(c, p, s):
                if isinstance(c, int):
                    setup(c, s, 0)
                if has(c, 1):
                    if s == 0:
                        dve.wait_ge(router_mm, c)
                        v.tensor_scalar(neglog[:, :], ps_b[:, 0:2 * NE], -1.0, None, ALU.mult).then_inc(neg_ready, 1)
                    if s == 2:
                        gate_steps(c, range(0, 4))
                    if s == 3:
                        dve.wait_ge(sig_ready, c)
                        v.scalar_tensor_tensor(flat(shared[:, :, :]), flat(shared[:, :, :]), 1.0, ps_c[:, :],
                                               ALU.add, ALU.mult).then_inc(sa_ready, 1)
                    if s == 4:
                        dve.wait_ge(sw3_mm, c)
                        dve.wait_ge(sa_ready, c)
                        v.tensor_tensor(flat(shared[:, :, :]), flat(shared[:, :, :]), ps_b[:, :],
                                        ALU.mult).then_inc(shared_ready, 1)
                    if s == 6:
                        dve.wait_ge(gelu_ready, 2 * c - 1)
                        gate_half(c, 0)
                    if s == 7:
                        gate_half(c, 1)
                if has(c, 2):
                    if s == 0:
                        dve.wait_ge(moe_mm, c - 1)
                        v.scalar_tensor_tensor(x1[:, :], ps_a[:, 0:CB], 1.0 / 6.0, x0[p][:, :], ALU.mult,
                                               ALU.add).then_inc(x1_ready, 1)
                    if s == 1:
                        masked(c, u_mm, um_ready)

            def slot_b(c, p, s):
                if isinstance(c, int):
                    setup(c, s, 1)
                if has(c, 2):
                    if s == 3:
                        masked(c, v_product_mm, vm_ready)
                    if s == 4:
                        dve.wait_ge(ada_mm, c - 1)
                        need(dve, y_ready, c - 3)
                        v.scalar_tensor_tensor(x2[p][:, :], x1[:, :], 2.0, ps_a[:, 0:CB], ALU.mult,
                                               ALU.add).then_inc(x2_ready, 1)
                if has(c, 1):
                    if s == 0:
                        dve.wait_ge(x0_hi_ready, c)
                        v.tensor_tensor(x0_lo[:, :], x0[1 - p][:, :], x0_hi[:, :].bitcast(f32),
                                        ALU.subtract).then_inc(x0_lo_ready, 1)
                    if s == 2:
                        gate_steps(c, range(4, 8))
                    if s == 3:
                        gate_steps(c, range(8, 12))
                    if s == 4:
                        gate_steps(c, range(12, GATE_STEPS))
                if s == ST - 1 and has(c, 0):
                    dve.wait_ge(h_ready, c * ST + ST)
                    v.scalar_tensor_tensor(x0[p][:, :], hist[p][:, :], 0.5, xin[p][:, :], ALU.mult,
                                           ALU.add).then_inc(x0_ready, 1)

            def iteration(h, p):
                c = 2 * h + p
                for s in range(ST):
                    g = c * ST + s
                    before = hist[p][:, cols(s - 1)] if s else hist[1 - p][:, cols(ST - 1)]
                    if has(c, 0):
                        dve.wait_ge(r_ready, g + 1)
                        v.scalar_tensor_tensor(rh[:, :], rgate[:, :], 1.0, before, ALU.add,
                                               ALU.mult).then_inc(rh_ready, 1)
                        dve.wait_ge(z_ready, g + 1)
                        v.scalar_tensor_tensor(keep[:, :], zgate[:, :], 1.0, before, ALU.subtract,
                                               ALU.mult).then_inc(keep_ready, 1)
                    slot_a(c, p, s)
                    if has(c, 0):
                        dve.wait_ge(keep_ready, g + 1)
                        dve.wait_ge(cand_ready, g + 1)
                        v.scalar_tensor_tensor(take[:, :], zgate[:, :], 1.0, cand[:, :], ALU.add,
                                               ALU.mult).then_inc(take_ready, 1)
                        dve.wait_ge(take_ready, g + 1)
                        v.scalar_tensor_tensor(hist[p][:, cols(s)], keep[:, :], -0.5, take[:, :], ALU.mult,
                                               ALU.add).then_inc(h_ready, 1)
                    slot_b(c, p, s)

            run_iterations(iteration, dve)


_INPUTS = ["x_t", "gru_pack", "add_rows", "cond_nat", "moe_pack", "ada_pack", "w2_pack", "const_pack"]


def kernel(**inputs):
    import numpy as np
    import concourse.bacc as bacc
    from concourse import mybir as mb
    from concourse.bass_utils import run_bass_kernel_spmd

    a = {k: np.asarray(v) for k, v in inputs.items()}
    n = lambda layer, name: a[f"L{layer}_cond_{name}"]
    f32 = np.float32

    x_t = a["x"].transpose(2, 1, 0).reshape(D, T * B)
    cond_t = a["cond_1024"].T
    gru_pack = np.concatenate(
        [cond_t] * 3 + [n(0, "C_r"), n(0, "C_z"), n(0, "C"), n(1, "router_t_w").T,
                        n(0, "W_r"), n(0, "W_z"), n(0, "W"), n(0, "U_r"), n(0, "U_z"), n(0, "U")], axis=1)
    add_rows = np.concatenate([n(0, "b_r"), n(0, "b_z"), n(0, "b"), np.zeros(NE, f32), n(3, "b")])
    add_rows = np.broadcast_to(add_rows, (96, V_END))
    moe_pack = np.concatenate(
        [n(1, "sw1").T, n(1, "sw3").T, n(1, "rw1").reshape(NE * HR, D).T,
         n(1, "sw2").T.reshape(2, 128, D).transpose(1, 0, 2).reshape(128, 2 * D),
         n(1, "rw2").transpose(0, 2, 1).reshape(NE // 2, 2 * HR, D).transpose(1, 0, 2).reshape(128, NE // 2 * D),
         n(1, "router_w").T, np.broadcast_to(np.tile(n(1, "router_bias"), 2), (128, 2 * NE))], axis=1)
    ada_pack = np.concatenate(
        [n(2, "base_down"), n(2, "base_up").T, n(2, "W1"), n(2, "ln_gamma")[:, None], n(2, "ln_beta")[:, None],
         n(2, "bias1")[:, None], n(2, "bias2").reshape(4, D, R).transpose(1, 0, 2).reshape(D, 4 * R),
         n(3, "Wx"), n(3, "Wh")], axis=1)
    w2_pack = n(2, "W2").reshape(D, 4, D, R).transpose(0, 1, 3, 2)

    hot = np.zeros((128, CB), f32)
    for part in range(3):
        hot[part * B:(part + 1) * B] = np.tile(np.eye(B, dtype=f32), (1, ST))
    mask = np.repeat(np.eye(GB, dtype=f32), R, axis=0)
    lower = np.tril(np.ones((NE, NE), f32), -1).reshape(1, NE * NE)
    const_pack = np.concatenate([np.eye(128, dtype=f32), hot, mask, np.broadcast_to(lower, (128, NE * NE))], axis=1)

    values = dict(x_t=x_t, gru_pack=gru_pack, add_rows=add_rows, cond_nat=a["cond_1024"], moe_pack=moe_pack,
                  ada_pack=ada_pack, w2_pack=w2_pack, const_pack=const_pack)
    nc = bacc.Bacc("TRN2", target_bir_lowering=False, num_devices=1)
    arrays, args = {}, []
    for name in _INPUTS:
        v = np.ascontiguousarray(values[name])
        arrays[name + "_dram"] = v
        args.append(nc.dram_tensor(name + "_dram", v.shape, mb.dt.from_np(v.dtype), kind="ExternalInput").ap())
    args.append(nc.dram_tensor("out_dram", (D, T * B), mb.dt.float32, kind="ExternalOutput").ap())
    recurrent_stack_kernel(nc, *args)
    r = run_bass_kernel_spmd(nc, [arrays], core_ids=[0])
    return np.ascontiguousarray(np.asarray(r.results[0]["out_dram"]).reshape(D, T, B).transpose(2, 1, 0))
```

```python
import concourse.bass as bass
from concourse import mybir
from contextlib import ExitStack

B, T, D = 32, 128, 128
NE, HR, HS = 8, 64, 256
R = 8
ST = 8
NC = T // ST
CB = ST * B
GB = 16
ROUTER_EPS = 1e-9
LN_EPS = 1e-5
EULER = 2.718281828459045

V_R, V_Z, V_H, V_T, V_B, V_END = 0, 128, 256, 384, 392, 520
G_COND = 0
G_C = 96
G_W = G_C + 392
G_U = G_W + 384
G_END = G_U + 384
M_SW1, M_SW3, M_RW1, M_SW2, M_RW2, M_RT, M_RB = 0, 256, 512, 1024, 1280, 1792, 1800
M_END = M_RB + 16
A_DOWN, A_UP, A_W1, A_GAMMA, A_BETA, A_BIAS1, A_BIAS2, A_WX, A_WH = 0, 128, 256, 384, 385, 386, 387, 419, 547
A_END = A_WH + 128
K_ID, K_HOT, K_MASK, K_LT = 0, 128, 128 + CB, 128 + CB + GB
K_END = K_LT + NE * NE
A1, B1, A2, B2 = range(4)


def recurrent_stack_kernel(nc, x_t, gru_pack, add_rows, cond_nat, moe_pack, ada_pack, w2_pack, const_pack, out_t):
    f32, bf16, f32r = mybir.dt.float32, mybir.dt.bfloat16, mybir.dt.float32r
    ALU, ACT, AX = mybir.AluOpType, mybir.ActivationFunctionType, mybir.AxisListType

    ctx = ExitStack()
    with ctx:
        def sb(name, shape, dt=f32):
            return ctx.enter_context(nc.sbuf_tensor(name, shape, dt))

        def bank(name):
            return ctx.enter_context(nc.psum_tensor(name, [128, 512], f32))

        def sem(name):
            return ctx.enter_context(nc.semaphore(name))

        gru = sb("gru", [128, G_END])
        rows = sb("rows", [96, V_END])
        cond = sb("cond", [B, D])
        moe = sb("moe", [128, M_END])
        ada = sb("ada", [128, A_END])
        w2 = sb("w2", [128, 4, R, D])
        const = sb("const", [128, K_END])
        ident = const[:, K_ID:K_ID + 128]
        hot = sb("hot", [96, CB], bf16)
        vparts = sb("vparts", [96, V_END], bf16)
        vres = sb("vres", [96, V_END])
        vtop = sb("vtop", [96, V_END], bf16)
        gate_hi, gate_lo = sb("gate_hi", [128, 3 * D], f32r), sb("gate_lo", [128, 3 * D], f32r)
        up_hi, up_lo = sb("up_hi", [128, M_SW2], f32r), sb("up_lo", [128, M_SW2], f32r)
        base_hi, base_lo = sb("base_hi", [128, 2 * D], f32r), sb("base_lo", [128, 2 * D], f32r)
        sw2_hi, sw2_lo = sb("sw2_hi", [128, 2 * D], f32r), sb("sw2_lo", [128, 2 * D], f32r)
        shared_hi, shared_lo = sb("shared_hi", [128, 2, CB], f32r), sb("shared_lo", [128, 2, CB], f32r)
        x1_hi, x1_lo = sb("x1_hi", [128, CB], f32r), sb("x1_lo", [128, CB], f32r)
        mid_hi, mid_lo = sb("mid_hi", [128, CB], f32r), sb("mid_lo", [128, CB], f32r)
        x_hi, x_lo = sb("x_hi", [128, CB], f32r), sb("x_lo", [128, CB], f32r)
        x0_hi, x0_lo = sb("x0_hi", [128, CB], f32r), sb("x0_lo", [128, CB], f32r)
        filler = sb("filler", [128, 256], bf16)
        adapt = sb("adapt", [128, 4, B, R])
        adapt_t = sb("adapt_t", [128, 2, 2, 128])
        u_scaled = sb("u_scaled", [128, 3 * D])
        table_load = sb("table_load", [1, 1])
        euler, ones_wide = sb("euler", [128, 2 * NE]), sb("ones_wide", [128, 2 * NE])
        neglog, expneg = sb("neglog", [128, 2 * NE]), sb("expneg", [128, 2, 2 * NE])
        t_term = sb("t_term", [128, 2 * NE])
        lnbuf = sb("lnbuf", [B, 3, D])
        lnstat = sb("lnstat", [B, 8])
        adah = sb("adah", [128, 2, B])
        xin = [sb(f"xin{p}", [128, CB]) for p in range(2)]
        hist = [sb(f"hist{p}", [128, CB]) for p in range(2)]
        x0 = [sb(f"x0_{p}", [128, CB]) for p in range(2)]
        x1 = sb("x1", [128, CB])
        x2 = [sb(f"x2_{p}", [128, CB]) for p in range(2)]
        rnn = [sb(f"rnn{p}", [128, CB]) for p in range(2)]
        yout = [sb(f"yout{p}", [128, CB]) for p in range(2)]
        rgate, zgate, cand = sb("rgate", [128, B]), sb("zgate", [128, B]), sb("cand", [128, B])
        rh, keep, take = sb("rh", [128, B]), sb("keep", [128, B]), sb("take", [128, B])
        shared = sb("shared", [128, 2, CB])
        hid = sb("hid", [128, 4, CB])
        sel = sb("sel", [128, 3, 2, NE])
        pair = sb("pair", [128, 3, 2, NE, NE])
        gst = sb("gst", [128, 6, 2])
        gmask = sb("gmask", [128, 4, 2, NE])
        gates = sb("gates", [128, 2, NE])
        gates_wide = [sb(f"gates_wide{k}", [128, 2, NE // 2, HR]) for k in range(2)]
        proj = sb("proj", [128, 2, ST, GB])
        mid = sb("mid", [128, CB])

        ps_rh = [bank(f"ps_rh{p}") for p in range(2)]
        ps_z = [bank(f"ps_z{p}") for p in range(2)]
        ps_n = bank("ps_n")
        ps_a, ps_b, ps_c = bank("ps_a"), bank("ps_b"), bank("ps_c")

        s_cond_w, s_gru, s_rows, s_cond, s_moe, s_ada, s_const, s_h30 = (
            sem(n) for n in ("cond_weights_loaded", "gru_loaded", "rows_loaded", "cond_loaded", "moe_loaded",
                             "ada_loaded", "const_loaded", "rnn_start_loaded"))
        s_w2 = [sem(f"w2_loaded{m}") for m in range(4)]
        x_loaded = [sem(f"x_loaded{p}") for p in range(2)]
        y_stored = [sem(f"y_stored{p}") for p in range(2)]
        s_hot, h_zero, s_half = (sem(n) for n in ("hot_ready", "h_start_ready", "half_ready"))
        v_mm, setup_chain, v_ready = sem("v_matmul_done"), sem("setup_chain"), sem("v_parts_ready")
        v_mid_ready, gate_hi_ready, gate_lo_ready, up_hi_ready, up_lo_ready, s_fill = (sem(n) for n in (
            "v_middle_ready", "gate_w_high", "gate_w_low", "up_w_high_half", "up_w_low_half", "filler_ready"))
        ln_dve, ln_pow, ln_tp = sem("ln_dve"), sem("ln_rsqrt_done"), sem("ln_transposed")
        c_ready, h2_mm, h2_ready = (sem(n) for n in ("ln_out_ready", "ada_hidden_mm", "ada_hidden_ready"))
        w_mm, w_out, t_mm, t_out, u_ready = (sem(n) for n in (
            "adapter_mm", "adapter_ready", "adapter_transposed", "adapter_t_ready", "u_scaled_ready"))
        LN_VAR, LN_OUT = 6, 7
        sw2_hi_ready, sw2_lo_ready = sem("sw2_high"), sem("sw2_low")
        base_hi_ready, base_lo_ready = sem("base_w_high"), sem("base_w_low")
        t_term_mm, t_term_ready = sem("t_term_mm"), sem("t_term_ready")
        r_mm, z_mm, c_mm = sem("reset_mm"), sem("update_mm"), sem("cand_mm")
        r_ready, z_ready, cand_ready = sem("reset_ready"), sem("update_ready"), sem("cand_ready")
        rh_ready, take_ready, h_ready = (sem(n) for n in ("reset_h_ready", "take_ready", "h_ready"))
        n_mm, n_ready = sem("rnn_mm"), sem("rnn_ready")
        x_hi_ready, x_lo_ready, x0_hi_ready, x0_lo_ready = (sem(n) for n in ("x_high", "x_low", "x0_high", "x0_low"))
        shared_hi_ready, shared_lo_ready = sem("shared_hidden_high"), sem("shared_hidden_low")
        x1_hi_ready, x1_lo_ready, mid_hi_ready, mid_lo_ready = (sem(n) for n in (
            "x1_high", "x1_low", "mid_high", "mid_low"))
        x0_ready, router_mm, neg_ready, exp_ready, sum_ready, gate_chain, gates_ready = (sem(n) for n in (
            "x0_ready", "router_mm", "neg_logits_ready", "exp_ready", "exp_plus_one_ready", "gates_chain",
            "gates_ready"))
        sw1_mm, sw3_mm, sig_ready, sa_ready, shared_ready = (sem(n) for n in (
            "sw1_mm", "sw3_mm", "sigmoid_ready", "silu_ready", "shared_hidden_ready"))
        even_ready = sem("even_gates_ready")
        wide_ready = sem("gates_wide_half")
        rw1_mm, gelu_ready, gate_tp, hid_ready = (sem(n) for n in (
            "rw1_mm_half", "gelu_half", "gates_transposed_half", "hidden_block"))
        moe_mm, x1_ready = sem("moe_out_mm"), sem("x1_ready")
        u_mm, um_ready, pre_mm, mid_ready = (sem(n) for n in (
            "u_mm", "u_masked", "mid_pre_mm", "mid_ready"))
        v_product_mm, vm_ready, ada_mm, x2_ready, y_ready = (sem(n) for n in (
            "v_mm_done", "v_masked", "adapter_out_mm", "x2_ready", "y_ready"))

        moe_half, x1_half, u_mm_half, um_half, pre_half, mid_half, v_mm_half, vm_half, ada_half, x2_half, y_last = (
            sem(n) for n in ("moe_out_half", "x1_half", "u_mm_half", "u_masked_half", "mid_pre_half", "mid_half",
                             "v_mm_half", "v_masked_half", "adapter_out_half", "x2_half", "y_last_step"))

        mask = const[:, K_MASK:K_MASK + GB]
        lt = const[:, K_LT:K_LT + NE * NE].rearrange("p (e j) -> p e j", e=NE)

        def cols(s, n=1):
            return slice(s * B, (s + n) * B)

        score, biased, rank = sel[:, 0], sel[:, 1], sel[:, 2]
        by_e = biased.unsqueeze(3).broadcast_to([128, 2, NE, NE])
        by_j = biased.unsqueeze(2).broadcast_to([128, 2, NE, NE])
        above, at_least, beats = pair[:, 0], pair[:, 1], pair[:, 2]
        chosen, picked, scaled_gates, even_gates = (gmask[:, n] for n in range(4))
        den, den_eps, rden, ok, scale, other = (gst[:, n] for n in range(6))

        def wide(a):
            return a.unsqueeze(2).broadcast_to([128, 2, NE])

        MOE_BANKS, RNN_BANKS = (ps_a, ps_z[1]), (ps_n, ps_a)

        def has(c, lag):
            return not isinstance(c, int) or 0 <= c - lag < NC

        FIRST_LOOP, LAST_LOOP = 5, 14
        LAST = NC - 1
        HALF = (slice(0, CB // 2), slice(CB // 2, CB))
        HG = CB // 4
        ADAPTER_MM = (0, 0, 0, 0, 2, 3, 2, 2, 2, 3, 2, 4, 2, 4, 2, 4)
        EVACUATE = ((0, 4, 0), (0, 6, 0), (0, 7, 0), (1, 0, 0))
        WARM_START, WARM_SPLIT, WARM = 16, 22, ((4, 5), (0, 3), (1, 2))
        GATE_STEPS, OTHER = 17, 13
        RNN_EARLY = 3

        def RNN_STEP(c, s):
            return c * ST + (s + RNN_EARLY - 3 * ST)


        def run_iterations(iteration, eng):
            for c in range(FIRST_LOOP):
                iteration(c // 2, c % 2)
            with eng.Fori(0, (LAST_LOOP + 1 - FIRST_LOOP) // 2) as i:
                iteration(i + FIRST_LOOP // 2, 1)
                iteration(i + (FIRST_LOOP + 1) // 2, 0)
            iteration(LAST // 2, LAST % 2)

        def need(eng, semaphore, count):
            if not isinstance(count, int) or count > 0:
                eng.wait_ge(semaphore, count)

        def of_parity(h, p, lag):
            return h + (p - lag) // 2 + 1

        block = ctx.enter_context(nc.Block())

        @block.sync
        def _(sp):
            sp.dma_start(gru[:, 0:G_W], gru_pack[:, 0:G_W]).then_inc(s_cond_w, 16)
            sp.dma_start(xin[0][:, :], x_t[:, 0:CB]).then_inc(x_loaded[0], 16)
            sp.dma_start(gru[:, G_W:G_END], gru_pack[:, G_W:G_END]).then_inc(s_gru, 16)
            sp.dma_start(xin[1][:, :], x_t[:, CB:2 * CB]).then_inc(x_loaded[1], 16)
            sp.dma_start(rnn[1][:, cols(ST - 1)], gru_pack[:, 0:B]).then_inc(s_h30, 16)
            sp.dma_start(ada[:, :], ada_pack).then_inc(s_ada, 16)
            for m in range(4):
                sp.dma_start(w2[:, m], w2_pack[:, m]).then_inc(s_w2[m], 16)
            sp.dma_start(moe[:, :], moe_pack).then_inc(s_moe, 16)

            def iteration(h, p):
                c = 2 * h + p
                if has(c, -1) and not (isinstance(c, int) and c == 0):
                    sp.wait_ge(x0_ready, c)
                    sp.dma_start(xin[1 - p][:, :], x_t[:, bass.ds(c * CB + CB, CB)]).then_inc(x_loaded[1 - p], 16)
                if has(c, 3):
                    sp.wait_ge(y_ready, c - 2)
                    sp.dma_start(out_t[:, bass.ds((c - 3) * CB, CB)], yout[1 - p][:, :]).then_inc(y_stored[1 - p], 16)

            run_iterations(iteration, sp)
            iteration(NC // 2, 0)
            iteration(NC // 2, 1)
            for count_of, steps in ((y_ready, slice(0, CB - B)), (y_last, slice(CB - B, CB))):
                sp.wait_ge(count_of, NC if count_of is y_ready else 1)
                sp.dma_start(out_t[:, LAST * CB + steps.start:LAST * CB + steps.stop],
                             yout[1][:, steps]).then_inc(y_stored[1], 16)
            sp.wait_ge(y_stored[0], 16 * (NC // 2))
            sp.wait_ge(y_stored[1], 16 * (NC // 2 + 1))

        @block.gpsimd
        def _(pool):
            def low_x(k, p):
                pool.wait_ge(x_hi_ready, k + 1)
                pool.tensor_tensor(x_lo[:, :], xin[p][:, :], x_hi[:, :].bitcast(f32),
                                   ALU.subtract).then_inc(x_lo_ready, 1)

            pool.memset(filler[:, :], 0.0).then_inc(s_fill, 1)
            pool.memset(hist[1][:, cols(ST - 1)], 0.0).then_inc(h_zero, 1)
            pool.memset(lnstat[:, 5:6], -0.5).then_inc(s_half, 1)
            pool.memset(euler[:, :], EULER).then_inc(s_half, 1)
            pool.memset(ones_wide[:, :], 1.0).then_inc(s_half, 1)
            pool.wait_ge(ln_dve, LN_VAR)
            pool.wait_ge(s_half, 3)
            pool.tensor_tensor(lnstat[:, 4:5], lnstat[:, 3:4], lnstat[:, 5:6], ALU.pow).then_inc(ln_pow, 1)
            low_x(0, 0)
            pool.wait_ge(s_gru, 16)
            pool.tensor_scalar(u_scaled[:, 0:2 * D], gru[:, G_U:G_U + 2 * D], 0.5, None, ALU.mult).then_inc(u_ready, 1)
            pool.tensor_scalar(u_scaled[:, 2 * D:3 * D], gru[:, G_U + 2 * D:G_END], 0.25, None,
                               ALU.mult).then_inc(u_ready, 1)
            pool.wait_ge(gate_hi_ready, 1)
            pool.tensor_tensor(gate_lo[:, :], gru[:, G_W:G_U], gate_hi[:, :].bitcast(f32),
                               ALU.subtract).then_inc(gate_lo_ready, 1)

            def iteration(h, p):
                c = 2 * h + p
                if has(c, 1):
                    pool.wait_ge(neg_ready, c)
                    pool.tensor_tensor(expneg[:, 0, :], euler[:, :], neglog[:, :], ALU.pow).then_inc(exp_ready, 1)
                    pool.wait_ge(exp_ready, c)
                    pool.tensor_tensor(expneg[:, 1, :], expneg[:, 0, :], ones_wide[:, :], ALU.add).then_inc(sum_ready, 1)
                if has(c, 0) and has(c, -1):
                    low_x(c + 1, 1 - p)
                if has(c, 2) and not (isinstance(c, int) and c == LAST + 2):
                    pool.wait_ge(mid_hi_ready, c - 1)
                    pool.tensor_tensor(mid_lo[:, :], mid[:, :], mid_hi[:, :].bitcast(f32),
                                       ALU.subtract).then_inc(mid_lo_ready, 1)
                if has(c, 1) and not (isinstance(c, int) and c == NC):
                    pool.wait_ge(shared_hi_ready, c)
                    pool.tensor_tensor(shared_lo[:, :, :], shared[:, :, :], shared_hi[:, :, :].bitcast(f32),
                                       ALU.subtract).then_inc(shared_lo_ready, 1)
                if has(c, 1):
                    pool.wait_ge(gate_chain, (c - 1) * (GATE_STEPS - 1) + OTHER + 1)
                    pool.tensor_tensor(even_gates, chosen, wide(other), ALU.mult).then_inc(even_ready, 1)
                if has(c, 3):
                    pool.wait_ge(x2_ready, c - 2)
                    pool.wait_ge(n_ready, c * ST - 2 * ST)
                    need(pool, y_stored[1 - p], 16 * of_parity(h, p, 5))
                    pool.tensor_tensor(yout[1 - p][:, :], x2[1 - p][:, :], rnn[1 - p][:, :],
                                       ALU.add).then_inc(y_ready, 1)

            run_iterations(iteration, pool)
            iteration(NC // 2, 0)
            iteration(NC // 2, 1)
            pool.wait_ge(x2_half, 2)
            pool.wait_ge(n_ready, T - 1)
            pool.wait_ge(y_stored[1], 16 * (NC // 2 - 1))
            pool.tensor_tensor(yout[1][:, 0:CB - B], x2[1][:, 0:CB - B], rnn[1][:, 0:CB - B],
                               ALU.add).then_inc(y_ready, 1)

        @block.tensor
        def _(pe):
            mm = nc.tensor.matmul

            def keep_warm(n, bank_of_zeros=ps_n):
                for _ in range(n):
                    mm(bank_of_zeros[:, 0:256], filler[:, 0:128], filler[:, :], start=True, stop=True)

            pe.wait_ge(s_fill, 1)
            keep_warm(WARM_START)
            pe.wait_ge(s_cond_w, 16)
            mm(ps_b[0:96, 0:V_B], gru[:, G_COND:G_COND + 96], gru[:, G_C:G_C + V_B], start=True,
               stop=True).then_inc(v_mm, 1)
            keep_warm(WARM_SPLIT // 2)
            pe.wait_ge(ln_dve, LN_OUT)
            pe.wait_ge(s_const, 16)
            nc.tensor.transpose(ps_c[:, 0:B], lnbuf[:, 2, :], ident[0:B, 0:B]).then_inc(ln_tp, 1)
            keep_warm(WARM_SPLIT // 2)

            def high_product(out, w, s_hi, first):
                mm(out, w, s_hi, start=first, stop=False, skip_group_check=True)

            def high_products(out, w_hi, w_lo, s_hi, first):
                high_product(out, w_hi, s_hi, first)
                high_product(out, w_lo, s_hi, False)

            def low_product(out, w_hi, s_lo):
                return mm(out, w_hi, s_lo, start=False, stop=True, skip_group_check=True)

            def per_batch_terms(out, v, first):
                mm(out, vparts[:, v:v + 128], hot[:, :], start=first, stop=False, skip_group_check=True)

            def project_low(out, n):
                low_product(out, gate_hi[:, n * 128:(n + 1) * 128], x_lo[:, :])

            def gate_u(n):
                return u_scaled[:, n * 128:(n + 1) * 128]

            def project_r_terms(p):
                per_batch_terms(ps_rh[1 - p][:, 0:CB], V_R, True)

            def project_r(c, p):
                pe.wait_ge(x_hi_ready, c + 2)
                per_batch_terms(ps_rh[1 - p][:, CB:2 * CB], V_H, False)
                high_products(ps_rh[1 - p][:, 0:CB], gate_hi[:, 0:D], gate_lo[:, 0:D], x_hi[:, :], False)

            def project_h(p):
                w = slice(2 * D, 3 * D)
                high_products(ps_rh[1 - p][:, CB:2 * CB], gate_hi[:, w], gate_lo[:, w], x_hi[:, :], False)

            def project_rh_low(c, p):
                pe.wait_ge(x_lo_ready, c + 2)
                project_low(ps_rh[1 - p][:, 0:CB], 0)
                project_low(ps_rh[1 - p][:, CB:2 * CB], 2)

            def project_z(p):
                out, w = ps_z[1 - p][:, 0:CB], slice(D, 2 * D)
                per_batch_terms(out, V_Z, True)
                high_products(out, gate_hi[:, w], gate_lo[:, w], x_hi[:, :], False)
                project_low(out, 1)

            def adapter_mm(part_rank):
                m, r = divmod(part_rank, R)
                bank_m = (ps_a, ps_b, ps_c, ps_a)[m]
                if part_rank == 0:
                    pe.wait_ge(h2_ready, 1)
                if r == 0:
                    pe.wait_ge(s_w2[m], 16)
                if part_rank == 3 * R:
                    pe.wait_ge(w_out, 1)
                last = mm(bank_m[:, r * B:(r + 1) * B], w2[:, m, r, :], adah[:, 1, :], start=True, stop=True)
                if r == R - 1:
                    last.then_inc(w_mm, 1)

            def setup(c, s, slot):
                if c < 2:
                    keep_warm(WARM[c if c or s < 2 else 2][slot])
                if (c, s, slot) == (0, 0, 1):
                    pe.wait_ge(c_ready, 1)
                    mm(ps_c[:, 0:B], ada[:, A_W1:A_W1 + D], adah[:, 0, :], start=True, stop=True).then_inc(h2_mm, 1)
                if c == 0:
                    first = sum(ADAPTER_MM[:2 * s + slot])
                    for part_rank in range(first, first + ADAPTER_MM[2 * s + slot]):
                        adapter_mm(part_rank)
                if (c, s, slot) == (0, 7, 0):
                    pe.wait_ge(v_ready, 4)
                    pe.wait_ge(w_out, 2)
                    for k in range(2):
                        last = mm(ps_b[:, k * NE:(k + 1) * NE], hot[:, k * 128:(k + 1) * 128],
                                  vparts[:, V_T:V_T + NE], start=True, stop=True)
                    last.then_inc(t_term_mm, 1)
                if (c, s, slot) == (1, 1, 0):
                    pe.wait_ge(w_out, 4)
                    for k, m in enumerate((A1, B2)):
                        for g in range(2):
                            last = nc.tensor.transpose(ps_a[:, (2 * k + g) * 128:(2 * k + g + 1) * 128],
                                                       adapt[:, m, g * GB:(g + 1) * GB, :], ident)
                    last.then_inc(t_mm, 1)

            def group(t, g):
                return t.rearrange("p (t b) -> p t b", b=B)[:, :, g * GB:(g + 1) * GB]

            def down_high(c):
                if isinstance(c, int) and c == 2:
                    pe.wait_ge(base_lo_ready, 1)
                pe.wait_ge(x1_hi_ready, c - 1)
                high_products(ps_a[:, 0:CB], base_hi[:, 0:D], base_lo[:, 0:D], x1_hi[:, :], True)

            def down_low(c):
                pe.wait_ge(x1_lo_ready, c - 1)
                low_product(ps_a[:, 0:CB], base_hi[:, 0:D], x1_lo[:, :])

            def low_rank(part, src, first):
                for g in range(2):
                    last = mm(ps_a[:, CB + g * 128:CB + (g + 1) * 128], adapt[:, part, g * GB:(g + 1) * GB, :],
                              group(src[:, :], g), start=(first and g == 0), stop=True, skip_group_check=True)
                return last

            def u_product():
                low_rank(A2, x1, False).then_inc(u_mm, 1)

            def v_product(c):
                pe.wait_ge(mid_ready, c - 1)
                low_rank(B1, mid, True)

            def add_low_rank(c, masked, k, done):
                pe.wait_ge(masked, c - 1)
                for g in range(2):
                    last = mm(group(ps_a[:, 0:CB], g), adapt_t[:, k, g, :], proj[:, g], start=False, stop=True,
                              skip_group_check=True)
                last.then_inc(done, 1)

            def up_product_of_mid(c):
                w = slice(D, 2 * D)
                pe.wait_ge(mid_hi_ready, c - 1)
                high_products(ps_a[:, 0:CB], base_hi[:, w], base_lo[:, w], mid_hi[:, :], False)
                pe.wait_ge(mid_lo_ready, c - 1)
                low_product(ps_a[:, 0:CB], base_hi[:, w], mid_lo[:, :]).then_inc(v_product_mm, 1)

            def router(c, p):
                pe.wait_ge(x0_ready, c)
                if isinstance(c, int) and c == 1:
                    pe.wait_ge(s_moe, 16)
                    pe.wait_ge(t_term_ready, 1)
                for k in range(2):
                    last = mm(ps_b[:, k * NE:(k + 1) * NE], x0[1 - p][:, k * 128:(k + 1) * 128],
                              moe[:, M_RT:M_RT + NE], start=True, stop=True)
                last.then_inc(router_mm, 1)

            def up_high(out, part, k):
                w = slice(k * 128, (k + 1) * 128)
                high_products(out[:, part * CB:(part + 1) * CB], up_hi[:, w], up_lo[:, w], x0_hi[:, :], part == 0)

            def up_low(out, part, k):
                return low_product(out[:, part * CB:(part + 1) * CB], up_hi[:, k * 128:(k + 1) * 128], x0_lo[:, :])

            def gates_by_row(half):
                out, wide = (ps_c, ps_b)[half], gates_wide[half]
                for k in range(2):
                    for tile in range(2):
                        last = nc.tensor.transpose(
                            out[:, k * CB + tile * 128:k * CB + (tile + 1) * 128],
                            wide[:, tile, 2 * k:2 * k + 2, :], ident)
                last.then_inc(gate_tp, 1)

            def moe_down(k, half, banks=(ps_a, ps_a)):
                col, src = (M_SW2 + k * 128, shared[:, k]) if k < 2 else (M_RW2 + (k - 2) * 128, hid[:, k - 2])
                part = slice(half * 128, (half + 1) * 128)
                first = k == 0 and (half == 0 or banks[0] is not banks[1])
                return mm(banks[half][:, part], moe[:, col:col + 128], src[:, part], start=first,
                          stop=(k == 5), skip_group_check=True)

            def shared_down(k, pieces):
                w = slice(k * D, (k + 1) * D)
                for piece in pieces:
                    mm(ps_a[:, 0:CB], (sw2_hi, sw2_lo, sw2_hi)[piece][:, w],
                       (shared_hi, shared_hi, shared_lo)[piece][:, k], start=(k == 0 and piece == 0),
                       stop=False, skip_group_check=True)

            def slot_a(h, p, c, s):
                if isinstance(c, int):
                    setup(c, s, 0)
                if has(c, -1):
                    if s == 2:
                        project_r_terms(p)
                    if s == 5:
                        project_z(p)
                if has(c, 2):
                    if s == 5:
                        need(pe, n_ready, c * ST - 2 * ST)
                        rnn_bias(slice(0, CB))
                    if s == 0:
                        moe_down(5, 1).then_inc(moe_mm, 1)
                    if s == 1:
                        down_low(c)
                        u_product()
                    if s == 3:
                        up_product_of_mid(c)
                if has(c, 1):
                    if s == 0:
                        router(c, p)
                    if s == 2:
                        up_low(ps_b, 0, 2)
                        up_high(ps_b, 1, 3)
                        up_low(ps_b, 1, 3).then_inc(sw3_mm, 1)
                    if s == 3:
                        pe.wait_ge(sa_ready, c)
                        up_high(ps_c, 0, 4)
                    if s == 4:
                        pe.wait_ge(shared_ready, c)
                        up_high(ps_b, 0, 6)
                        up_high(ps_b, 1, 7)
                        up_low(ps_b, 0, 6)
                    if s == 6:
                        pe.wait_ge(wide_ready, 2 * c - 1)
                        pe.wait_ge(gelu_ready, 2 * c - 1)
                        gates_by_row(0)
                        shared_down(1, (0,))
                    if s == 7:
                        pe.wait_ge(hid_ready, 4 * c - 3)
                        moe_down(2, 0)
                        moe_down(2, 1)
                        pe.wait_ge(hid_ready, 4 * c - 2)
                        moe_down(3, 0)

            def rnn_step(q, k, step, out=ps_n):
                before = rnn[q][:, cols(k - 1)] if k else rnn[1 - q][:, cols(ST - 1)]
                need(pe, n_ready, step)
                if isinstance(step, int) and step == 0:
                    pe.wait_ge(s_h30, 16)
                mm(out[:, cols(k)], ada[:, A_WH:A_WH + D], before, start=False, stop=True,
                   skip_group_check=True).then_inc(n_mm, 1)

            def rnn_bias(part, out=ps_n):
                mm(out[:, part], vparts[:, V_B:V_END], hot[:, part], start=True, stop=False,
                   skip_group_check=True)

            def rnn_input(q, part, out=ps_n):
                mm(out[:, part], ada[:, A_WX:A_WX + D], x2[q][:, part], start=False, stop=True,
                   skip_group_check=True)

            def second_recurrence(c, p, s):
                if s == ST - RNN_EARLY and has(c, 2):
                    pe.wait_ge(x2_ready, c - 1)
                    rnn_input(p, slice(0, CB))
                if has(c, 3 if s < ST - RNN_EARLY else 2):
                    k = (s + RNN_EARLY) % ST
                    q = p if s >= ST - RNN_EARLY else 1 - p
                    rnn_step(q, k, RNN_STEP(c, s))

            def slot_b(h, p, c, s):
                if isinstance(c, int):
                    setup(c, s, 1)
                if s != ST - RNN_EARLY:
                    second_recurrence(c, p, s)
                if has(c, 1):
                    if s == 0:
                        if isinstance(c, int) and c == 1:
                            pe.wait_ge(up_lo_ready, 2)
                        pe.wait_ge(x0_hi_ready, c)
                        up_high(ps_c, 0, 0)
                        up_high(ps_c, 1, 1)
                        pe.wait_ge(neg_ready, c)
                        high_product(ps_b[:, 0:CB], up_hi[:, 2 * D:3 * D], x0_hi[:, :], True)
                    if s == 1:
                        pe.wait_ge(x0_lo_ready, c)
                        up_low(ps_c, 0, 0)
                        up_low(ps_c, 1, 1).then_inc(sw1_mm, 1)
                        high_product(ps_b[:, 0:CB], up_lo[:, 2 * D:3 * D], x0_hi[:, :], False)
                    if s == 3:
                        up_high(ps_c, 1, 5)
                        up_low(ps_c, 0, 4)
                        up_low(ps_c, 1, 5).then_inc(rw1_mm, 1)
                    if s == 4:
                        up_low(ps_b, 1, 7).then_inc(rw1_mm, 1)
                    if s == 5:
                        need(pe, x2_ready, c - 1)
                        if isinstance(c, int) and c == 1:
                            pe.wait_ge(sw2_lo_ready, 1)
                        pe.wait_ge(shared_hi_ready, c)
                        shared_down(0, (0, 1))
                        pe.wait_ge(shared_lo_ready, c)
                        shared_down(0, (2,))
                    if s == 6:
                        shared_down(1, (1, 2))
                        pe.wait_ge(wide_ready, 2 * c)
                        pe.wait_ge(gelu_ready, 2 * c)
                        gates_by_row(1)
                    if s == 7:
                        moe_down(3, 1)
                        pe.wait_ge(hid_ready, 4 * c - 1)
                        moe_down(4, 0)
                        moe_down(4, 1)
                        pe.wait_ge(hid_ready, 4 * c)
                        moe_down(5, 0)
                if has(c, 2):
                    if s == 0:
                        down_high(c)
                    if s == 1:
                        if isinstance(c, int) and c == 2:
                            pe.wait_ge(t_out, 1)
                        add_low_rank(c, um_ready, 1, pre_mm)
                    if s == 2:
                        v_product(c)
                    if s == 4:
                        add_low_rank(c, vm_ready, 0, ada_mm)
                if has(c, -1):
                    if s == 2:
                        project_r(c, p)
                    if s == 3:
                        project_h(p)
                    if s == 4:
                        project_rh_low(c, p)
                if s == ST - RNN_EARLY:
                    second_recurrence(c, p, s)

            pe.wait_ge(v_ready, 2)
            pe.wait_ge(s_hot, 1)
            pe.wait_ge(gate_lo_ready, 1)
            project_r_terms(1)
            project_r(-1, 1)
            project_h(1)
            project_rh_low(-1, 1)
            project_z(1)

            def iteration(h, p):
                c = 2 * h + p
                for s in range(ST):
                    before = hist[p][:, cols(s - 1)] if s else hist[1 - p][:, cols(ST - 1)]
                    if has(c, 0):
                        if isinstance(c, int) and c * ST + s == 0:
                            pe.wait_ge(h_zero, 1)
                            pe.wait_ge(u_ready, 2)
                        need(pe, h_ready, c * ST + s)
                        mm(ps_rh[p][:, cols(s)], gate_u(0), before, start=False, stop=True,
                           skip_group_check=True).then_inc(r_mm, 1)
                        mm(ps_z[p][:, cols(s)], gate_u(1), before, start=False, stop=True,
                           skip_group_check=True).then_inc(z_mm, 1)
                    slot_a(h, p, c, s)
                    if has(c, 0):
                        pe.wait_ge(rh_ready, c * ST + s + 1)
                        mm(ps_rh[p][:, CB + s * B:CB + (s + 1) * B], gate_u(2), rh[:, :], start=False, stop=True,
                           skip_group_check=True).then_inc(c_mm, 1)
                    slot_b(h, p, c, s)

            run_iterations(iteration, pe)

            def step(chunk, k):
                out = RNN_BANKS[k * 2 // ST] if chunk == LAST else ps_n
                rnn_step(chunk % 2, k, chunk * ST + k, out)

            c = NC
            moe_down(5, 1).then_inc(moe_mm, 1)
            router(c, 0)
            step(LAST - 2, 3)
            pe.wait_ge(x0_hi_ready, c)
            up_high(ps_c, 0, 0)
            up_high(ps_c, 1, 1)
            down_high(c)
            down_low(c)
            u_product()
            pe.wait_ge(x0_lo_ready, c)
            up_low(ps_c, 0, 0)
            up_low(ps_c, 1, 1).then_inc(sw1_mm, 1)
            pe.wait_ge(neg_ready, c)
            up_high(ps_b, 0, 2)
            up_high(ps_b, 1, 3)
            up_low(ps_b, 0, 2)
            up_low(ps_b, 1, 3).then_inc(sw3_mm, 1)
            step(LAST - 2, 4)
            add_low_rank(c, um_ready, 1, pre_mm)
            step(LAST - 2, 5)
            v_product(c)
            step(LAST - 2, 6)
            up_product_of_mid(c)
            for half, read_out in enumerate((sa_ready, shared_ready)):
                pe.wait_ge(read_out, c)
                out, k = (ps_c, ps_b)[half], 4 + 2 * half
                up_high(out, 0, k)
                up_high(out, 1, k + 1)
                up_low(out, 0, k)
                up_low(out, 1, k + 1).then_inc(rw1_mm, 1)
                if half == 0:
                    step(LAST - 2, 7)
                    add_low_rank(c, vm_ready, 0, ada_mm)
            pe.wait_ge(n_ready, LAST * ST - ST)
            rnn_bias(slice(0, CB))
            pe.wait_ge(x2_ready, c - 1)
            rnn_input(0, slice(0, CB))
            step(LAST - 1, 0)
            for k in range(2):
                for half in range(2):
                    moe_down(k, half, MOE_BANKS)
            step(LAST - 1, 1)
            for half in range(2):
                pe.wait_ge(wide_ready, 2 * c - 1 + half)
                pe.wait_ge(gelu_ready, 2 * c - 1 + half)
                gates_by_row(half)
            step(LAST - 1, 2)
            for half in range(2):
                for k in range(2, 6):
                    if half == 0:
                        pe.wait_ge(hid_ready, 4 * c - 3 + k - 2)
                    last = moe_down(k, half, MOE_BANKS)
                last.then_inc(moe_half, 1)
                step(LAST - 1, 3 + half)

            def low_rank_half(h, part, src, ready, done):
                pe.wait_ge(ready, h + 1)
                for g in range(2):
                    last = mm((ps_b, ps_c)[h][:, g * HG:(g + 1) * HG], adapt[:, part, g * GB:(g + 1) * GB, :],
                              group(src[:, HALF[h]], g), start=(g == 0), stop=True, skip_group_check=True)
                last.then_inc(done, 1)

            def add_half(h, base, k, masked_half, done):
                pe.wait_ge(masked_half, h + 1)
                for g in range(2):
                    last = mm(group(base[h][:, 0:CB // 2], g), adapt_t[:, k, g, :],
                              proj[:, g, h * ST // 2:(h + 1) * ST // 2], start=False, stop=True,
                              skip_group_check=True)
                last.then_inc(done, 1)

            def u_half(h):
                low_rank_half(h, A2, x1, x1_half, u_mm_half)
                mm(ps_rh[h][:, 0:CB // 2], ada[:, A_DOWN:A_DOWN + D], x1[:, HALF[h]], start=True, stop=False,
                   skip_group_check=True)

            def v_half(h):
                low_rank_half(h, B1, mid, mid_half, v_mm_half)
                mm(ps_z[h][:, 0:CB // 2], ada[:, A_UP:A_UP + D], mid[:, HALF[h]], start=True, stop=False,
                   skip_group_check=True)

            u_half(0)
            step(LAST - 1, 5)
            u_half(1)
            add_half(0, ps_rh, 1, um_half, pre_half)
            step(LAST - 1, 6)
            add_half(1, ps_rh, 1, um_half, pre_half)
            step(LAST - 1, 7)
            v_half(0)
            v_half(1)
            add_half(0, ps_z, 0, vm_half, ada_half)
            add_half(1, ps_z, 0, vm_half, ada_half)
            pe.wait_ge(n_ready, LAST * ST)
            rnn_bias(HALF[0])
            rnn_bias(HALF[1], RNN_BANKS[1])
            pe.wait_ge(x2_half, 1)
            rnn_input(1, HALF[0])
            step(LAST, 0)
            pe.wait_ge(x2_half, 2)
            rnn_input(1, HALF[1], RNN_BANKS[1])
            for k in range(1, ST):
                step(LAST, k)
                if k < ST - 1:
                    keep_warm(4, ps_rh[0])

        @block.scalar
        def _(act):
            act.dma_start(cond[:, :], cond_nat).then_inc(s_cond, 16)
            act.dma_start(rows[:, :], add_rows).then_inc(s_rows, 16)
            act.dma_start(const[:, :], const_pack).then_inc(s_const, 16)
            fn = nc.scalar.activation
            act.wait_ge(s_fill, 1)
            fn(table_load[:, :], filler[0:1, 0:1], ACT.Gelu)
            act.wait_ge(x_loaded[0], 16)
            fn(x_hi[:, :], xin[0][:, :], ACT.Copy).then_inc(x_hi_ready, 1)
            act.wait_ge(s_const, 16)
            fn(hot[:, :], const[0:96, K_HOT:K_HOT + CB], ACT.Copy).then_inc(s_hot, 1)
            act.wait_ge(s_gru, 16)
            fn(gate_hi[:, :], gru[:, G_W:G_U], ACT.Copy).then_inc(gate_hi_ready, 1)
            act.wait_ge(v_mid_ready, 1)
            fn(vparts[32:64, 0:V_T], vtop[32:64, 0:V_T], ACT.Copy).then_inc(v_ready, 1)

            def high_x0(c, p):
                act.wait_ge(x0_ready, c)
                fn(x0_hi[:, :], x0[1 - p][:, :], ACT.Copy).then_inc(x0_hi_ready, 1)

            def high_x1(c):
                act.wait_ge(x1_ready, c - 1)
                fn(x1_hi[:, :], x1[:, :], ACT.Copy).then_inc(x1_hi_ready, 1)

            def gelu_mid(c):
                act.wait_ge(pre_mm, c - 1)
                fn(mid[:, :], ps_a[:, 0:CB], ACT.Gelu).then_inc(mid_ready, 1)
                act.wait_ge(mid_ready, c - 1)
                fn(mid_hi[:, :], mid[:, :], ACT.Copy).then_inc(mid_hi_ready, 1)

            def tanh_w1(c):
                act.wait_ge(sw1_mm, c)
                fn(shared[:, :, :], ps_c[:, :].rearrange("p (k n) -> p k n", k=2),
                   ACT.Tanh, scale=0.5).then_inc(sig_ready, 1)

            def gelu_hidden(c, half):
                act.wait_ge(rw1_mm, 2 * c - 1 + half)
                fn(hid[:, 2 * half:2 * half + 2, :], (ps_c, ps_b)[half][:, :].rearrange(
                    "p (k n) -> p k n", k=2), ACT.Gelu).then_inc(gelu_ready, 1)

            def slot_a(c, p, s):
                if s == 0 and has(c, 1):
                    high_x0(c, p)
                if isinstance(c, int) and (c, s) == (0, 2):
                    act.wait_ge(v_mid_ready, 2)
                    fn(vparts[32:64, V_T:], vtop[32:64, V_T:], ACT.Copy).then_inc(v_ready, 1)
                if isinstance(c, int) and c == 0 and s in (4, 5):
                    if s == 4:
                        act.wait_ge(s_moe, 16)
                    part = slice((s - 4) * 512, (s - 3) * 512)
                    fn(up_hi[:, part], moe[:, part], ACT.Copy).then_inc(up_hi_ready, 1)
                if isinstance(c, int) and (c, s) == (0, 1):
                    act.wait_ge(h2_mm, 1)
                    fn(adah[:, 1, :], ps_c[:, 0:B], ACT.Gelu, bias=ada[:, A_BIAS1:A_BIAS1 + 1]).then_inc(h2_ready, 1)
                if s == 2 and has(c, 2):
                    gelu_mid(c)
                if s == 4 and has(c, 1):
                    act.wait_ge(shared_ready, c)
                    fn(shared_hi[:, :, :], shared[:, :, :], ACT.Copy).then_inc(shared_hi_ready, 1)
                if s == 6 and has(c, 1):
                    widen(c, 1)

            def widen(c, half):
                act.wait_ge(gates_ready, c)
                fn(gates_wide[half][:, :, :, :], gates[:, :, 4 * half:4 * half + 4].unsqueeze(3).broadcast_to(
                    [128, 2, NE // 2, HR]), ACT.Copy).then_inc(wide_ready, 1)

            def slot_b(h, c, p, s):
                if isinstance(c, int) and (c, s) == (1, 0):
                    fn(sw2_hi[:, :], moe[:, M_SW2:M_SW2 + 2 * D], ACT.Copy).then_inc(sw2_hi_ready, 1)
                    act.wait_ge(s_ada, 16)
                    fn(base_hi[:, :], ada[:, A_DOWN:A_DOWN + 2 * D], ACT.Copy).then_inc(base_hi_ready, 1)
                if s == 0 and has(c, 2):
                    high_x1(c)
                if has(c, 1):
                    if s == 1:
                        tanh_w1(c)
                    if s in (3, 4):
                        gelu_hidden(c, s - 3)
                    if s == 5:
                        widen(c, 0)
                if s == 1 and has(c, 0) and has(c, -1):
                    act.wait_ge(x_loaded[1 - p], 16 * of_parity(h, p, -1))
                    fn(x_hi[:, :], xin[1 - p][:, :], ACT.Copy).then_inc(x_hi_ready, 1)

            def rnn_tanh(q, k, step, src=ps_n):
                act.wait_ge(n_mm, step + 1)
                fn(rnn[q][:, cols(k)], src[:, cols(k)], ACT.Tanh).then_inc(n_ready, 1)

            def iteration(h, p):
                c = 2 * h + p
                for s in range(ST):
                    if has(c, 0):
                        act.wait_ge(r_mm, c * ST + s + 1)
                        fn(rgate[:, :], ps_rh[p][:, cols(s)], ACT.Tanh, scale=0.5).then_inc(r_ready, 1)
                        act.wait_ge(z_mm, c * ST + s + 1)
                        fn(zgate[:, :], ps_z[p][:, cols(s)], ACT.Tanh, scale=0.5).then_inc(z_ready, 1)
                    slot_a(c, p, s)
                    if has(c, 0):
                        act.wait_ge(c_mm, c * ST + s + 1)
                        fn(cand[:, :], ps_rh[p][:, CB + s * B:CB + (s + 1) * B], ACT.Tanh).then_inc(cand_ready, 1)
                    if s in (0, ST - RNN_EARLY):
                        slot_b(h, c, p, s)
                    if has(c, 3 if s < ST - RNN_EARLY else 2):
                        k = (s + RNN_EARLY) % ST
                        q = p if s >= ST - RNN_EARLY else 1 - p
                        if k == 0:
                            need(act, y_ready, c - 3)
                        rnn_tanh(q, k, RNN_STEP(c, s))
                    if s not in (0, ST - RNN_EARLY):
                        slot_b(h, c, p, s)

            run_iterations(iteration, act)

            def step(chunk, k):
                rnn_tanh(chunk % 2, k, chunk * ST + k, RNN_BANKS[k * 2 // ST] if chunk == LAST else ps_n)

            def gelu_mid_half(h):
                act.wait_ge(pre_half, h + 1)
                fn(mid[:, HALF[h]], ps_rh[h][:, 0:CB // 2], ACT.Gelu).then_inc(mid_half, 1)

            c = NC
            high_x0(c, 0)
            high_x1(c)
            step(LAST - 2, 3)
            tanh_w1(c)
            step(LAST - 2, 4)
            gelu_mid(c)
            step(LAST - 2, 5)
            step(LAST - 2, 6)
            gelu_hidden(c, 0)
            step(LAST - 2, 7)
            gelu_hidden(c, 1)
            step(LAST - 1, 0)
            widen(c, 0)
            widen(c, 1)
            for k in range(1, 6):
                step(LAST - 1, k)
            gelu_mid_half(0)
            step(LAST - 1, 6)
            gelu_mid_half(1)
            step(LAST - 1, 7)
            act.wait_ge(y_ready, NC - 2)
            for k in range(ST):
                step(LAST, k)

        @block.vector
        def _(dve):
            v = nc.vector
            links = [0]

            def link(ins):
                links[0] += 1
                ins.then_inc(setup_chain, 1)
                dve.wait_ge(setup_chain, links[0])

            dve.wait_ge(s_cond, 16)
            ln_count = [0]

            def ln(ins):
                ln_count[0] += 1
                ins.then_inc(ln_dve, 1)
                dve.wait_ge(ln_dve, ln_count[0])

            ln(v.reduce_sum(lnstat[:, 0:1], cond[:, :], axis=AX.X))
            ln(v.tensor_scalar(lnstat[:, 1:2], lnstat[:, 0:1], -1.0 / D, None, ALU.mult))
            ln(v.tensor_scalar(lnbuf[:, 0, :], cond[:, :], lnstat[:, 1:2], None, ALU.add))
            ln(v.tensor_tensor(lnbuf[:, 1, :], lnbuf[:, 0, :], lnbuf[:, 0, :], ALU.mult))
            ln(v.reduce_sum(lnstat[:, 2:3], lnbuf[:, 1, :], axis=AX.X))
            ln(v.tensor_scalar(lnstat[:, 3:4], lnstat[:, 2:3], 1.0 / D, LN_EPS, ALU.mult, ALU.add))
            assert ln_count[0] == LN_VAR
            dve.wait_ge(ln_pow, 1)
            ln(v.tensor_scalar(lnbuf[:, 2, :], lnbuf[:, 0, :], lnstat[:, 4:5], None, ALU.mult))
            assert ln_count[0] == LN_OUT

            def split_terms(part, steps):
                for n in steps:
                    if n == 0:
                        link(v.tensor_copy(vparts[:, part], rows[:, part]))
                    if n == 1:
                        link(v.tensor_tensor(vres[:, part], rows[:, part], vparts[:, part], ALU.subtract))
                    if n == 2:
                        v.tensor_copy(vtop[:, part], vres[:, part]).then_inc(v_mid_ready, 1)
                        dve.wait_ge(v_mid_ready, 1 if part.start == 0 else 2)
                        v.tensor_tensor(vparts[64:96, part], vres[64:96, part], vtop[64:96, part],
                                        ALU.subtract).then_inc(v_ready, 1)

            dve.wait_ge(s_rows, 16)
            dve.wait_ge(v_mm, 1)
            link(v.tensor_tensor(rows[:, 0:V_B], ps_b[0:96, 0:V_B], rows[:, 0:V_B], ALU.add))
            split_terms(slice(0, V_T), range(3))
            dve.wait_ge(ln_tp, 1)
            dve.wait_ge(s_ada, 16)
            v.tensor_scalar(adah[:, 0, :], ps_c[:, 0:B], ada[:, A_GAMMA:A_GAMMA + 1],
                            ada[:, A_BETA:A_BETA + 1], ALU.mult, ALU.add).then_inc(c_ready, 1)

            def setup(c, s, slot):
                if c == 0 and s in (0, 1) and slot:
                    split_terms(slice(V_T, V_END), ((0, 1), (2,))[s])
                if c == 0 and s in (5, 6) and slot:
                    part = slice((s - 5) * 512, (s - 4) * 512)
                    dve.wait_ge(up_hi_ready, s - 4)
                    v.tensor_tensor(up_lo[:, part], moe[:, part], up_hi[:, part].bitcast(f32),
                                    ALU.subtract).then_inc(up_lo_ready, 1)
                if (c, s, slot) == (0, 7, 1):
                    dve.wait_ge(t_term_mm, 1)
                    v.tensor_copy(t_term[:, :], ps_b[:, 0:2 * NE]).then_inc(t_term_ready, 1)
                if (c, s, slot) in EVACUATE:
                    m = EVACUATE.index((c, s, slot))
                    dve.wait_ge(w_mm, m + 1)
                    out = adapt[:, m].rearrange("p b r -> p r b")
                    bias = ada[:, A_BIAS2 + m * R:A_BIAS2 + (m + 1) * R].unsqueeze(2).broadcast_to([128, R, B])
                    v.tensor_tensor(out, (ps_a, ps_b, ps_c, ps_a)[m][:, 0:CB].rearrange("p (r b) -> p r b", b=B),
                                    bias, ALU.add).then_inc(w_out, 1)
                if (c, s, slot) == (1, 1, 1):
                    dve.wait_ge(sw2_hi_ready, 1)
                    v.tensor_tensor(sw2_lo[:, :], moe[:, M_SW2:M_SW2 + 2 * D], sw2_hi[:, :].bitcast(f32),
                                    ALU.subtract).then_inc(sw2_lo_ready, 1)
                if (c, s, slot) == (1, 5, 1):
                    dve.wait_ge(base_hi_ready, 1)
                    v.tensor_tensor(base_lo[:, :], ada[:, A_DOWN:A_DOWN + 2 * D], base_hi[:, :].bitcast(f32),
                                    ALU.subtract).then_inc(base_lo_ready, 1)
                if (c, s, slot) == (1, 1, 0):
                    dve.wait_ge(t_mm, 1)
                    v.tensor_copy(adapt_t[:, :, :, :].rearrange("p k g n -> p (k g n)"), ps_a[:, :]).then_inc(t_out, 1)

            def masked(c, done, out_sem):
                dve.wait_ge(done, c - 1)
                v.tensor_tensor(proj[:, :, :, :].rearrange("p g t b -> p (g t) b"),
                                ps_a[:, CB:2 * CB].rearrange("p (n b) -> p n b", b=GB),
                                mask.unsqueeze(1).broadcast_to([128, 2 * ST, GB]), ALU.mult).then_inc(out_sem, 1)

            def gate_steps(c, steps):
                done = (c - 1) * (GATE_STEPS - 1)

                def after(n):
                    dve.wait_ge(gate_chain, done + n + 1)

                for n in steps:
                    if n == 0:
                        dve.wait_ge(sum_ready, c)
                        ins = v.reciprocal(score, expneg[:, 1, :].rearrange("p (k e) -> p k e", k=2))
                    if n == 1:
                        after(0)
                        ins = v.tensor_tensor(biased, score, moe[:, M_RB:M_RB + 2 * NE].rearrange(
                            "p (k e) -> p k e", k=2), ALU.add)
                    if n == 2:
                        after(1)
                        ins = v.tensor_tensor(at_least, by_j, by_e, ALU.is_ge)
                    if n == 3:
                        ins = v.tensor_tensor(above, by_j, by_e, ALU.is_gt)
                    if n == 4:
                        after(2)
                        ins = v.tensor_tensor(at_least, at_least, lt.unsqueeze(1).broadcast_to([128, 2, NE, NE]),
                                              ALU.mult)
                    if n == 5:
                        after(4)
                        ins = v.tensor_tensor(beats, above, at_least, ALU.max)
                    if n == 6:
                        after(5)
                        ins = v.reduce_sum(rank, beats, axis=AX.X)
                    if n == 7:
                        after(6)
                        ins = v.tensor_scalar(chosen, rank, 2.0, None, ALU.is_lt)
                    if n == 8:
                        after(7)
                        ins = v.tensor_tensor(picked, chosen, score, ALU.mult)
                    if n == 9:
                        after(8)
                        ins = v.reduce_sum(den, picked, axis=AX.X)
                    if n == 10:
                        after(9)
                        ins = v.tensor_scalar(ok, den, ROUTER_EPS, 2.0, ALU.is_gt, ALU.mult)
                    if n == 11:
                        ins = v.tensor_scalar(den_eps, den, ROUTER_EPS, None, ALU.add)
                    if n == 12:
                        after(11)
                        ins = v.reciprocal(rden, den_eps)
                    if n == 13:
                        ins = v.tensor_scalar(other, ok, -0.5, 1.0, ALU.mult, ALU.add)
                    if n == 14:
                        after(12)
                        ins = v.tensor_tensor(scale, ok, rden, ALU.mult)
                    if n == 15:
                        after(14)
                        ins = v.tensor_tensor(scaled_gates, picked, wide(scale), ALU.mult)
                    if n == 16:
                        after(15)
                        dve.wait_ge(even_ready, c)
                        v.tensor_tensor(gates[:, :, :], scaled_gates, even_gates, ALU.add).then_inc(gates_ready, 1)
                    else:
                        ins.then_inc(gate_chain, 1)

            def flat(t):
                return t.rearrange("p k n -> p (k n)")

            def gate_rows(c, k):
                half, part = divmod(k, 2)
                if part == 0:
                    dve.wait_ge(gelu_ready, 2 * c - 1 + half)
                    dve.wait_ge(gate_tp, 2 * c - 1 + half)
                v.tensor_tensor(hid[:, k], hid[:, k], (ps_c, ps_b)[half][:, part * CB:(part + 1) * CB],
                                ALU.mult).then_inc(hid_ready, 1)

            def negate_logits(c):
                dve.wait_ge(router_mm, c)
                v.scalar_tensor_tensor(neglog[:, :], ps_b[:, 0:2 * NE], -1.0, t_term[:, :], ALU.mult,
                                       ALU.subtract).then_inc(neg_ready, 1)

            def low_x0(c, p):
                dve.wait_ge(x0_hi_ready, c)
                v.tensor_tensor(x0_lo[:, :], x0[1 - p][:, :], x0_hi[:, :].bitcast(f32),
                                ALU.subtract).then_inc(x0_lo_ready, 1)

            def low_x1(c):
                dve.wait_ge(x1_hi_ready, c - 1)
                v.tensor_tensor(x1_lo[:, :], x1[:, :], x1_hi[:, :].bitcast(f32),
                                ALU.subtract).then_inc(x1_lo_ready, 1)

            def silu_w1(c):
                dve.wait_ge(sig_ready, c)
                v.scalar_tensor_tensor(flat(shared[:, :, :]), flat(shared[:, :, :]), 1.0, ps_c[:, :],
                                       ALU.add, ALU.mult).then_inc(sa_ready, 1)

            def times_w3(c):
                dve.wait_ge(sw3_mm, c)
                dve.wait_ge(sa_ready, c)
                v.tensor_tensor(flat(shared[:, :, :]), flat(shared[:, :, :]), ps_b[:, :],
                                ALU.mult).then_inc(shared_ready, 1)

            def make_x1(part, p, src, done, count, ready):
                dve.wait_ge(done, count)
                v.scalar_tensor_tensor(x1[:, part], src[:, part], 1.0 / 6.0, x0[p][:, part], ALU.mult,
                                       ALU.add).then_inc(ready, 1)

            def make_x2(c, p):
                dve.wait_ge(ada_mm, c - 1)
                need(dve, y_ready, c - 3)
                v.scalar_tensor_tensor(x2[p][:, :], x1[:, :], 2.0, ps_a[:, 0:CB], ALU.mult,
                                       ALU.add).then_inc(x2_ready, 1)

            def slot_a(c, p, s):
                if isinstance(c, int):
                    setup(c, s, 0)
                if has(c, 2):
                    if s == 0:
                        make_x1(slice(0, CB), p, ps_a, moe_mm, c - 1, x1_ready)
                    if s == 1:
                        masked(c, u_mm, um_ready)
                if has(c, 1):
                    if s == 0:
                        negate_logits(c)
                    if s == 2:
                        gate_steps(c, range(0, 3))
                    if s == 3:
                        times_w3(c)
                    if s == 4:
                        gate_steps(c, range(6, 9))
                    if s == 5:
                        gate_steps(c, range(13, GATE_STEPS))
                    if s == 6:
                        gate_rows(c, 0)
                    if s == 7:
                        gate_rows(c, 3)

            def slot_b(c, p, s):
                if isinstance(c, int):
                    setup(c, s, 1)
                if has(c, 2):
                    if s == 3:
                        masked(c, v_product_mm, vm_ready)
                if s == 4 and has(c, 1):
                    gate_steps(c, range(9, 12))
                if s == 4 and has(c, 2):
                    make_x2(c, p)
                if s == 4 and has(c, 1):
                    gate_steps(c, range(12, 13))
                if s == 0 and has(c, 2):
                    low_x1(c)
                if has(c, 1):
                    if s == 0:
                        low_x0(c, p)
                    if s == 2:
                        silu_w1(c)
                        gate_steps(c, range(3, 4))
                    if s == 3:
                        gate_steps(c, range(4, 6))
                    if s == 6:
                        gate_rows(c, 1)
                        gate_rows(c, 2)
                if s == ST - 1 and has(c, 0):
                    dve.wait_ge(h_ready, c * ST + ST)
                    v.scalar_tensor_tensor(x0[p][:, :], hist[p][:, :], 0.5, xin[p][:, :], ALU.mult,
                                           ALU.add).then_inc(x0_ready, 1)

            def iteration(h, p):
                c = 2 * h + p
                for s in range(ST):
                    g = c * ST + s
                    before = hist[p][:, cols(s - 1)] if s else hist[1 - p][:, cols(ST - 1)]
                    if has(c, 0):
                        dve.wait_ge(r_ready, g + 1)
                        v.scalar_tensor_tensor(rh[:, :], rgate[:, :], 1.0, before, ALU.add,
                                               ALU.mult).then_inc(rh_ready, 1)
                        dve.wait_ge(z_ready, g + 1)
                        v.scalar_tensor_tensor(keep[:, :], zgate[:, :], 1.0, before, ALU.subtract, ALU.mult)
                    slot_a(c, p, s)
                    if has(c, 0):
                        dve.wait_ge(cand_ready, g + 1)
                        v.scalar_tensor_tensor(take[:, :], zgate[:, :], 1.0, cand[:, :], ALU.add,
                                               ALU.mult).then_inc(take_ready, 1)
                        dve.wait_ge(take_ready, g + 1)
                        v.scalar_tensor_tensor(hist[p][:, cols(s)], keep[:, :], -0.5, take[:, :], ALU.mult,
                                               ALU.add).then_inc(h_ready, 1)
                    slot_b(c, p, s)

            run_iterations(iteration, dve)

            c = NC
            make_x1(slice(0, CB), 0, ps_a, moe_mm, c - 1, x1_ready)
            negate_logits(c)
            low_x0(c, 0)
            low_x1(c)
            masked(c, u_mm, um_ready)
            silu_w1(c)
            times_w3(c)
            gate_steps(c, range(0, 5))
            masked(c, v_product_mm, vm_ready)
            gate_steps(c, range(5, 9))
            make_x2(c, 0)
            gate_steps(c, range(9, GATE_STEPS))
            for k in range(4):
                gate_rows(c, k)
            for h in range(2):
                make_x1(HALF[h], 1, MOE_BANKS[h], moe_half, h + 1, x1_half)

            def masked_half(h, done, ready):
                dve.wait_ge(done, h + 1)
                v.tensor_tensor(proj[:, :, h * ST // 2:(h + 1) * ST // 2, :],
                                (ps_b, ps_c)[h][:, 0:2 * HG].rearrange("p (g t b) -> p g t b", g=2, b=GB),
                                mask.unsqueeze(1).unsqueeze(1).broadcast_to([128, 2, ST // 2, GB]),
                                ALU.mult).then_inc(ready, 1)

            for h in range(2):
                masked_half(h, u_mm_half, um_half)
            for h in range(2):
                masked_half(h, v_mm_half, vm_half)
            for h in range(2):
                dve.wait_ge(ada_half, h + 1)
                dve.wait_ge(y_ready, NC - 2)
                v.scalar_tensor_tensor(x2[1][:, HALF[h]], x1[:, HALF[h]], 2.0, ps_z[h][:, 0:CB // 2], ALU.mult,
                                       ALU.add).then_inc(x2_half, 1)
            dve.wait_ge(y_stored[1], 16 * (NC // 2 - 1))
            dve.wait_ge(n_ready, T)
            dve.wait_ge(x2_half, 2)
            v.tensor_tensor(yout[1][:, CB - B:CB], x2[1][:, CB - B:CB], rnn[1][:, CB - B:CB],
                            ALU.add).then_inc(y_last, 1)


_INPUTS = ["x_t", "gru_pack", "add_rows", "cond_nat", "moe_pack", "ada_pack", "w2_pack", "const_pack"]


def kernel(**inputs):
    import numpy as np
    import concourse.bacc as bacc
    from concourse import mybir as mb
    from concourse.bass_utils import run_bass_kernel_spmd

    a = {k: np.asarray(v) for k, v in inputs.items()}
    n = lambda layer, name: a[f"L{layer}_cond_{name}"]
    f32 = np.float32

    x_t = a["x"].transpose(2, 1, 0).reshape(D, T * B)
    cond_t = a["cond_1024"].T
    gru_pack = np.concatenate(
        [cond_t] * 3 + [n(0, "C_r"), n(0, "C_z"), n(0, "C"), n(1, "router_t_w").T,
                        n(0, "W_r"), n(0, "W_z"), n(0, "W"), n(0, "U_r"), n(0, "U_z"), n(0, "U")], axis=1)
    add_rows = np.concatenate([n(0, "b_r"), n(0, "b_z"), n(0, "b"), np.zeros(NE, f32), n(3, "b")])
    add_rows = np.broadcast_to(add_rows, (96, V_END))
    moe_pack = np.concatenate(
        [n(1, "sw1").T, n(1, "sw3").T, n(1, "rw1").reshape(NE * HR, D).T,
         n(1, "sw2").T.reshape(2, 128, D).transpose(1, 0, 2).reshape(128, 2 * D),
         n(1, "rw2").transpose(0, 2, 1).reshape(NE // 2, 2 * HR, D).transpose(1, 0, 2).reshape(128, NE // 2 * D),
         n(1, "router_w").T, np.broadcast_to(np.tile(n(1, "router_bias"), 2), (128, 2 * NE))], axis=1)
    ada_pack = np.concatenate(
        [n(2, "base_down"), n(2, "base_up").T, n(2, "W1"), n(2, "ln_gamma")[:, None], n(2, "ln_beta")[:, None],
         n(2, "bias1")[:, None], n(2, "bias2").reshape(4, D, R).transpose(1, 0, 2).reshape(D, 4 * R),
         n(3, "Wx"), n(3, "Wh")], axis=1)
    w2_pack = n(2, "W2").reshape(D, 4, D, R).transpose(0, 1, 3, 2)

    hot = np.zeros((128, CB), f32)
    for part in range(3):
        hot[part * B:(part + 1) * B] = np.tile(np.eye(B, dtype=f32), (1, ST))
    mask = np.repeat(np.eye(GB, dtype=f32), R, axis=0)
    lower = np.tril(np.ones((NE, NE), f32), -1).reshape(1, NE * NE)
    const_pack = np.concatenate([np.eye(128, dtype=f32), hot, mask, np.broadcast_to(lower, (128, NE * NE))], axis=1)

    values = dict(x_t=x_t, gru_pack=gru_pack, add_rows=add_rows, cond_nat=a["cond_1024"], moe_pack=moe_pack,
                  ada_pack=ada_pack, w2_pack=w2_pack, const_pack=const_pack)
    nc = bacc.Bacc("TRN2", target_bir_lowering=False, num_devices=1)
    arrays, args = {}, []
    for name in _INPUTS:
        v = np.ascontiguousarray(values[name])
        arrays[name + "_dram"] = v
        args.append(nc.dram_tensor(name + "_dram", v.shape, mb.dt.from_np(v.dtype), kind="ExternalInput").ap())
    args.append(nc.dram_tensor("out_dram", (D, T * B), mb.dt.float32, kind="ExternalOutput").ap())
    recurrent_stack_kernel(nc, *args)
    r = run_bass_kernel_spmd(nc, [arrays], core_ids=[0])
    return np.ascontiguousarray(np.asarray(r.results[0]["out_dram"]).reshape(D, T, B).transpose(2, 1, 0))
```
